# Optimizing a Trainium2 kernel written in Bass

```python
import numpy as np
import jax
import jax.numpy as jnp

def _softmax(x, axis=-1):
    return jax.nn.softmax(x, axis=axis)

def _gelu(x):
    return jax.nn.gelu(x, approximate=True)

def _silu(x):
    return jax.nn.silu(x)

def _sigmoid(x):
    return jax.nn.sigmoid(x)

def _layernorm(x, axis=-1, eps=1e-05):
    m = jnp.mean(x, axis=axis, keepdims=True)
    v = jnp.var(x, axis=axis, keepdims=True)
    return (x - m) / jnp.sqrt(v + eps)

def _scatter_add(tgt, idx, src, axis=0):
    return tgt.at[idx].add(src)

def _segment_sum(src, seg, n):
    return jax.ops.segment_sum(src, seg, n)
kernel_name = 'mk_seq_postln_d1_jaxref_r4_b56138'

def setup_inputs(seed: int=0):
    np.random.seed(seed)
    _w = jnp.asarray

    def _L0_attn_setup():
        import jax, jax.numpy as jnp
        import numpy as np
        import math
        D_MODEL = 512
        NUM_HEADS = 16
        HEAD_DIM = D_MODEL // NUM_HEADS
        key = jax.random.key(seed)
        k_x, k_wqkv, k_bqkv, k_wo, k_bo = jax.random.split(key, 5)
        B, S = (2, 512)
        scale = 1.0 / math.sqrt(D_MODEL)
        return {'x': jax.random.normal(k_x, (B, S, D_MODEL), dtype=jnp.float32), 'w_qkv': jax.random.normal(k_wqkv, (3 * D_MODEL, D_MODEL), dtype=jnp.float32) * scale, 'b_qkv': jax.random.normal(k_bqkv, (3 * D_MODEL,), dtype=jnp.float32) * 0.01, 'w_out': jax.random.normal(k_wo, (D_MODEL, D_MODEL), dtype=jnp.float32) * scale, 'b_out': jax.random.normal(k_bo, (D_MODEL,), dtype=jnp.float32) * 0.01}
    _L0_attn_in = _L0_attn_setup()

    def _L0_ffn_setup():
        import jax, jax.numpy as jnp
        import numpy as np
        ZERO_POINT = 128.0

        def _dequant(wq, scale):
            return (wq.astype(jnp.float32) - ZERO_POINT) * scale[:, None]
        key = jax.random.key(seed)
        ks = jax.random.split(key, 7)
        H, I = (512, 2048)
        B, S = (2, 512)
        hidden_state = jax.random.normal(ks[0], (B, S, H), dtype=jnp.float32)
        gate_w = jax.random.randint(ks[1], (I, H), 0, 64, dtype=jnp.int32)
        up_w = jax.random.randint(ks[2], (I, H), 0, 64, dtype=jnp.int32)
        down_w = jax.random.randint(ks[3], (H, I), 0, 64, dtype=jnp.int32)
        gate_scale = jax.random.uniform(ks[4], (I,), dtype=jnp.float32) * 0.02
        up_scale = jax.random.uniform(ks[5], (I,), dtype=jnp.float32) * 0.02
        down_scale = jax.random.uniform(ks[6], (H,), dtype=jnp.float32) * 0.02
        return {'hidden_state': hidden_state, 'gate_w': gate_w, 'gate_scale': gate_scale, 'up_w': up_w, 'up_scale': up_scale, 'down_w': down_w, 'down_scale': down_scale}
    _L0_ffn_in = _L0_ffn_setup()
    _d = {'L0_attn_x': _L0_attn_in['x'], 'L0_attn_w_qkv': _L0_attn_in['w_qkv'], 'L0_attn_b_qkv': _L0_attn_in['b_qkv'], 'L0_attn_w_out': _L0_attn_in['w_out'], 'L0_attn_b_out': _L0_attn_in['b_out'], 'L0_ffn_gate_w': _L0_ffn_in['gate_w'], 'L0_ffn_gate_scale': _L0_ffn_in['gate_scale'], 'L0_ffn_up_w': _L0_ffn_in['up_w'], 'L0_ffn_up_scale': _L0_ffn_in['up_scale'], 'L0_ffn_down_w': _L0_ffn_in['down_w'], 'L0_ffn_down_scale': _L0_ffn_in['down_scale']}
    _x0 = _d['L0_attn_x']
    _d['L0_attn_x'] = jax.random.normal(jax.random.fold_in(jax.random.key(seed), 1), (4, 512, 512), dtype=_x0.dtype)
    del _x0
    return _d

def reference(L0_attn_x, L0_attn_w_qkv, L0_attn_b_qkv, L0_attn_w_out, L0_attn_b_out, L0_ffn_gate_w, L0_ffn_gate_scale, L0_ffn_up_w, L0_ffn_up_scale, L0_ffn_down_w, L0_ffn_down_scale):

    def _L0_attn_ref(x, w_qkv, b_qkv, w_out, b_out):
        import jax, jax.numpy as jnp
        import numpy as np
        import math
        D_MODEL = 512
        NUM_HEADS = 16
        HEAD_DIM = D_MODEL // NUM_HEADS
        B, S, D = x.shape
        H, Hd = (NUM_HEADS, HEAD_DIM)
        qkv = jnp.einsum('bsd,ed->bse', x, w_qkv) + b_qkv
        qkv = qkv.reshape(B, S, 3, H, Hd)
        q = jnp.transpose(qkv[:, :, 0], (0, 2, 1, 3))
        k = jnp.transpose(qkv[:, :, 1], (0, 2, 1, 3))
        v = jnp.transpose(qkv[:, :, 2], (0, 2, 1, 3))
        scores = jnp.einsum('bhqd,bhkd->bhqk', q, k) / math.sqrt(Hd)
        causal = jnp.triu(jnp.full((S, S), -jnp.inf, dtype=scores.dtype), k=1)
        scores = scores + causal[None, None]
        attn = jax.nn.softmax(scores, axis=-1)
        out = jnp.einsum('bhqk,bhkd->bhqd', attn, v)
        out = jnp.transpose(out, (0, 2, 1, 3)).reshape(B, S, D)
        return jnp.einsum('bsd,ed->bse', out, w_out) + b_out

    def _L0_ffn_ref(hidden_state, gate_w, gate_scale, up_w, up_scale, down_w, down_scale):
        import jax, jax.numpy as jnp
        import numpy as np
        ZERO_POINT = 128.0

        def _dequant(wq, scale):
            return (wq.astype(jnp.float32) - ZERO_POINT) * scale[:, None]
        Wg = _dequant(gate_w, gate_scale)
        Wu = _dequant(up_w, up_scale)
        Wd = _dequant(down_w, down_scale)
        g = jnp.einsum('bsh,ih->bsi', hidden_state, Wg)
        u = jnp.einsum('bsh,ih->bsi', hidden_state, Wu)
        h = jax.nn.silu(g) * u
        return jnp.einsum('bsi,hi->bsh', h, Wd)
    x = L0_attn_x
    x = _layernorm(x + _L0_attn_ref(x, L0_attn_w_qkv, L0_attn_b_qkv, L0_attn_w_out, L0_attn_b_out), axis=-1)
    x = _layernorm(x + _L0_ffn_ref(x, L0_ffn_gate_w, L0_ffn_gate_scale, L0_ffn_up_w, L0_ffn_up_scale, L0_ffn_down_w, L0_ffn_down_scale), axis=-1)
    return x

_drawn_inputs = setup_inputs


def setup_inputs(seed=0):
    import zlib

    import numpy as np

    out = dict(_drawn_inputs(seed))
    spreads = {}
    factors = {}
    for name, (base, spread) in spreads.items():
        noise = np.random.default_rng([zlib.crc32(name.encode()), seed]).standard_normal(out[name].shape)
        drawn = base * np.exp(spread * noise) if base else spread * noise
        out[name] = jnp.asarray(drawn.astype(out[name].dtype))
    for name, factor in factors.items():
        out[name] = (out[name] * factor).astype(out[name].dtype)
    return out
```

```python
import concourse.bass as bass
from concourse import mybir
from contextlib import ExitStack


def postln_block_kernel(nc: bass.Bass, x, w_qkv, b_qkv, w_out, b_out, gate_w, gate_scale, up_w, up_scale,
                        down_w, down_scale, out):
    F32, F32R, I32 = mybir.dt.float32, mybir.dt.float32r, mybir.dt.int32
    ALU, ACT = mybir.AluOpType, mybir.ActivationFunctionType

    P = 128
    B, S, D = x.shape
    HD = 32
    H = D // HD
    I = gate_w.shape[0]
    ND = D // P
    NT = S // P
    NI = I // P
    HG = P // HD
    NG = H // HG
    NE = 3 * D
    SLOTS = HG * NT
    SCALE = float(HD) ** -0.5
    EPS = 1e-5
    ZERO_POINT = 128.0
    FLOOR = -3.0e38
    TPR = 4
    NROUND = (NE + D) // (P * TPR)
    STAT = 3 * HD
    STACK_DMAS = 6 * 16

    FRONT = ([("x", c) for c in range(ND)] + [("q", 0), ("k", 0)] + [("v", t) for t in range(NT)] +
             [("q", 1), ("k", 1), ("m", 0)])

    def batch_jobs(ahead):
        jobs = []
        for g in range(NG):
            if ahead and g == NG - 2:
                jobs += [("x", c) for c in range(2, ND)]
            if ahead or g + 2 < NG:
                jobs += [("q", g + 2), ("k", g + 2)]
            if ahead or g + 1 < NG:
                jobs += [("m", g + 1)]
            if ahead and g == NG - 3:
                jobs += [("x", c) for c in range(2)]
        return jobs + [("v", t) for t in range(NT) if ahead] + [("o", t) for t in range(NT)]

    PER_BATCH = len(batch_jobs(True))
    assert PER_BATCH % 2 == 0

    class Jobs:

        def __init__(self, b, jobs, before):
            self.b, self.before = b, before
            self.place = {job: before + n for n, job in enumerate(jobs)}

        def bank(self, *job):
            return self.place[job] % 2

        def done(self, *job):
            return self.b * (PER_BATCH // 2) + self.place[job] // 2 + 1

        def before_it(self, *job):
            return None if self.place[job] < 2 else self.done(*job) - 1

    front_jobs = Jobs(0, FRONT, 0)

    def jobs_of(b, ahead):
        return Jobs(b, batch_jobs(ahead), len(FRONT))

    y1_dram = nc.dram_tensor("y1_scratch", (B * S, D), F32, kind="Internal").ap()
    x_v = x.rearrange("b (t p) d -> b p t d", p=P)
    y1_v = y1_dram.rearrange("(b t p) d -> b p t d", p=P, t=NT)
    out_v = out.rearrange("b (t p) d -> b p t d", p=P)
    gate_v = gate_w.rearrange("(r s p) d -> r p s d", p=P, s=TPR)
    up_v = up_w.rearrange("(r s p) d -> r p s d", p=P, s=TPR)
    down_v = down_w.rearrange("(t p) (s c) -> t p s c", p=P, c=D)

    def of_batch(view, b):
        return view[bass.ds(b, 1)].rearrange("o p t d -> (o p) t d")

    ctx = ExitStack()
    with ctx:
        def sb(name, shape, dt=F32, where=ctx):
            return where.enter_context(nc.sbuf_tensor(name, shape, dt))

        def sem(name):
            return ctx.enter_context(nc.semaphore(name))

        def sem_pair(name):
            return [sem(f"{name}{i}") for i in range(2)]

        ident = sb("ident", [P, P])
        x_tok = sb("x_tok", [P, NT, D])
        xT_hi = sb("xT_hi", [P, ND, S], F32R)
        xT_lo = sb("xT_lo", [P, ND, S], F32R)
        z_tok = sb("z_tok", [P, NT, D])
        ln_stat = sb("ln_stat", [P, NT, 6])
        ln_mv = sb("ln_mv", [P, NT, 2])
        ln_var = sb("ln_var", [P, NT])
        ln_rstd = sb("ln_rstd", [P, NT])
        half_power = sb("half_power", [P, NT])

        att = ExitStack()
        wT_hi = sb("wT_hi", [P, ND, NE + D], F32R, att)
        wT_lo = sb("wT_lo", [P, ND, NE + D], F32R, att)
        q_stack = [sb(f"q_stack{i}", [P, HG, S], F32R, att) for i in range(2)]
        k_stack = [sb(f"k_stack{i}", [P, HG, S], F32R, att) for i in range(2)]
        q_hi = sb("q_hi", [P, S], F32R, att)
        q_lo = sb("q_lo", [P, S], F32R, att)
        k_hi = sb("k_hi", [P, S], F32R, att)
        k_lo = sb("k_lo", [P, S], F32R, att)
        v_tok = sb("v_tok", [P, NT, D], F32, att)
        attT_hi = sb("attT_hi", [P, NG, S], F32R, att)
        attT_lo = sb("attT_lo", [P, NG, S], F32R, att)
        attT = sb("attT", [P, S], F32, att)
        log_sum = sb("log_sum", [P, S], F32, att)
        inv_est = sb("inv_est", [P, S], F32, att)
        inv_err = sb("inv_err", [P, S], F32, att)
        neg_inv = sb("neg_inv", [P, S], F32, att)
        masked = sb("masked", [P, 2, S], mybir.dt.bfloat16, att)
        causal = sb("causal", [P, S], F32, att)
        ones = sb("ones", [P, HD], F32, att)
        row_max = sb("row_max", [P, NT, HG], F32, att)
        neg_max = sb("neg_max", [P, NT, 2, HG], F32R, att)
        max_rows = sb("max_rows", [2 * HG, S], F32R, att)
        bias_qk = sb("bias_qk", [P, 2 * NG], F32, att)
        bias_v = sb("bias_v", [P, D], F32, att)
        bias_o = sb("bias_o", [P, D], F32, att)
        P_WIDTH = [S - kb * P for kb in range(NT)]
        P_FIRST = [HG * sum(P_WIDTH[:kb]) for kb in range(NT)]
        probs_sb = sb("probs_sb", [P, HG * sum(P_WIDTH)], F32, att)
        probs = [probs_sb[:, P_FIRST[kb]:P_FIRST[kb] + HG * P_WIDTH[kb]].rearrange("p (j q) -> p j q", j=HG)
                 for kb in range(NT)]
        w_stage = [t.rearrange("p (s d) -> p s d", s=TPR) for t in
                   (probs_sb[:, 0:TPR * D], probs_sb[:, TPR * D:2 * TPR * D])] + [z_tok[:, :, :]]
        att.close()

        ffn = ExitStack()
        gateT = sb("gateT", [P, ND, I], F32R, ffn)
        upT = sb("upT", [P, ND, I], F32R, ffn)
        downT = sb("downT", [P, NI, D], F32R, ffn)
        w_int = sb("w_int", [P, 2, TPR, D], I32, ffn)
        w_shift = sb("w_shift", [P, 2, D], F32, ffn)
        silu = sb("silu", [P, 2, S], F32, ffn)
        hid = sb("hid", [P, 2, S], F32, ffn)
        hid_hi = sb("hid_hi", [P, 2, S], F32R, ffn)
        hid_lo = sb("hid_lo", [P, 2, S], F32R, ffn)
        d_scaled = sb("d_scaled", [P, 2, D], F32, ffn)
        g_scale = sb("g_scale", [P, NI], F32, ffn)
        u_scale = sb("u_scale", [P, NI], F32, ffn)
        d_scale = sb("d_scale", [P, D], F32, ffn)
        ffn.close()

        bank = [ctx.enter_context(nc.psum_tensor(f"bank{i}", [P, 512], F32)) for i in range(8)]
        pj, score, scoreT, pv_acc, sum_acc = bank[0:2], bank[2:4], bank[4:6], bank[6], bank[7]
        gate_acc, up_acc, down_acc = bank[0:2], bank[2:4], bank[4:8]
        y_bank = [gate_acc[0], up_acc[0], gate_acc[1], up_acc[1]]

        consts_ready = sem("consts_ready")
        pool_step = sem("pool_step")
        bias_loaded = sem("bias_loaded")
        w_loaded = [sem(f"w_loaded{r}") for r in range(NROUND)]
        w_full = sem("w_full")
        w_hi_done = sem("w_hi_done")
        w_free = sem("w_free")
        x_loaded = sem("x_loaded")
        z_loaded = sem("z_loaded")
        res_ready = sem("res_ready")
        pj_full = sem_pair("pj_full")
        pj_drained = sem_pair("pj_drained")
        x_hi_done = sem("x_hi_done")
        qk_hi_done = sem("qk_hi_done")
        stacked = sem("stacked")
        stacks_set = sem("stacks_set")
        score_full = sem("score_full")
        max_done = sem("max_done")
        max_hi_done = sem("max_hi_done")
        max_split = sem("max_split")
        max_placed = sem("max_placed")
        scoreT_full = sem("scoreT_full")
        exp_done = sem("exp_done")
        probs_masked = sem("probs_masked")
        pv_full = sem("pv_full")
        log_done = sem("log_done")
        est_done = sem("est_done")
        err_done = sem("err_done")
        inv_done = sem("inv_done")
        att_done = sem("att_done")
        att_hi_done = sem("att_hi_done")
        att_ready = sem("att_ready")
        z_done = sem("z_done")
        stat_done = sem("stat_done")
        mv_done = sem("mv_done")
        var_done = sem("var_done")
        rstd_done = sem("rstd_done")
        y1_done = sem("y1_done")
        y1_stored = sem("y1_stored")
        scales_loaded = sem("scales_loaded")
        fw_loaded = sem_pair("fw_loaded")
        fw_shifted = sem("fw_shifted")
        fw_full = sem("fw_full")
        fw_free = [sem("fw_free_act"), sem("fw_free_dve")]
        y_loaded = sem("y_loaded")
        r_loaded = sem("r_loaded")
        yT_full = sem("yT_full")
        yT_hi_done = sem("yT_hi_done")
        yT_done = sem("yT_done")
        gate_full = sem("gate_full")
        up_full = sem("up_full")
        silu_done = sem("silu_done")
        hid_done = sem("hid_done")
        hid_hi_done = sem("hid_hi_done")
        hid_ready = sem("hid_ready")
        down_full = sem("down_full")
        d_done = sem("d_done")
        z2_done = sem("z2_done")
        stat2_done = sem("stat2_done")
        mv2_done = sem("mv2_done")
        var2_done = sem("var2_done")
        rstd2_done = sem("rstd2_done")
        out_done = sem("out_done")
        out_stored = sem("out_stored")

        NFW = 2 * NI + ND * NI // TPR
        FW_ROUNDS = NFW // TPR

        def wait_alone(eng, sem, value):
            value = eng.to_reg(value) if not isinstance(value, int) else value
            eng.wait_ge(consts_ready, 1)
            eng.wait_ge(sem, value)

        def ffn_weight_place(n):
            if n < NI:
                return gateT[:, :, n * P:(n + 1) * P]
            if n < 2 * NI:
                return upT[:, :, (n - NI) * P:(n - NI + 1) * P]
            t, s = divmod(n - 2 * NI, TPR)
            return downT[:, TPR * s:TPR * (s + 1), t * P:(t + 1) * P]

        def evict_ffn_weight(eng, n, copy):
            eng.wait_ge(fw_full, n + 1)
            copy(ffn_weight_place(n), pj[n % 2][:, :].rearrange("p (c e) -> p c e", c=TPR)).then_inc(fw_free[n % 2], 1)

        def shift_ffn_weight(dve, n):
            r, s = divmod(n, TPR)
            dve.wait_ge(fw_loaded[r % 2], 16 * (r // 2 + 1))
            if n >= 2:
                dve.wait_ge(fw_full, n - 1)
            nc.vector.tensor_scalar(w_shift[:, n % 2, :], w_int[:, r % 2, s, :], -ZERO_POINT, None,
                                    ALU.add).then_inc(fw_shifted, 1)

        def by_row(wT, first):
            return wT[:, :, bass.ds(first, P)].rearrange("p c (d j) -> p c j d", j=HG)

        block = ctx.enter_context(nc.Block())

        @block.sync
        def _(sp):
            def load_w(r):
                src = w_qkv[r * TPR * P:(r + 1) * TPR * P, :] if r < NE // (TPR * P) else w_out
                sp.dma_start(w_stage[r % 3], src.rearrange("(s p) d -> p s d", p=P)).then_inc(w_loaded[r], 16)

            for r in range(3):
                load_w(r)
            sp.dma_start(x_tok[:, :, :], x_v[0]).then_inc(x_loaded, 16)
            with nc.allow_non_contiguous_dma(reason="a bias per partition"):
                for j in range(HG):
                    sp.dma_start(bias_qk[j:P:HG, :],
                                 b_qkv[0:2 * D].rearrange("(c j d) -> j d c", j=HG, d=HD)[j]).then_inc(bias_loaded, 16)
            sp.dma_start(bias_v[:, :], b_qkv[2 * D:3 * D].partition_broadcast(P)).then_inc(bias_loaded, 16)
            sp.dma_start(bias_o[:, :], b_out.partition_broadcast(P)).then_inc(bias_loaded, 16)
            sp.wait_ge(w_full, TPR)
            load_w(3)
            sp.wait_ge(w_full, 3 * TPR)
            sp.dma_start(z_tok[:, :, :], x_v[0]).then_inc(z_loaded, 16)

            def stack(jobs, b, r):
                wait_alone(sp, pj_drained[jobs.bank("k", r)], jobs.done("k", r))
                if r >= 2:
                    wait_alone(sp, scoreT_full, b * (NG * SLOTS) + (r - 1) * SLOTS)
                for n, (qs, ks) in enumerate(((q_hi, k_hi), (q_hi, k_lo), (q_lo, k_hi))):
                    to = slice(HD * n, HD * (n + 1))
                    sp.dma_start(q_stack[r % 2][to, :, :].bitcast(F32), qs[:, :].bitcast(F32)).then_inc(stacked, 16)
                    sp.dma_start(k_stack[r % 2][to, :, :].bitcast(F32), ks[:, :].bitcast(F32)).then_inc(stacked, 16)

            def place_max(jobs, r):
                wait_alone(sp, pj_drained[jobs.bank("m", r)], jobs.done("m", r))
                sp.dma_start(q_stack[r % 2][STAT:STAT + 2, :, :].bitcast(F32),
                             max_rows[:, :].bitcast(F32)).then_inc(max_placed, 16)

            stack(front_jobs, 0, 0)
            stack(front_jobs, 0, 1)
            place_max(front_jobs, 0)

            def batch(b, ahead):
                jobs = jobs_of(b, ahead)
                if ahead:
                    sp.dma_start(x_tok[:, :, :], of_batch(x_v, b + 1)).then_inc(x_loaded, 16)
                for g in range(NG):
                    if ("m", g + 1) in jobs.place:
                        place_max(jobs, g + 1)
                    if ("k", g + 2) in jobs.place:
                        stack(jobs, b, g + 2)
                for t in range(NT):
                    wait_alone(sp, y1_done, b * NT + t + 1)
                    sp.dma_start(of_batch(y1_v, b)[:, t, :], z_tok[:, t, :]).then_inc(y1_stored, 16)
                if ahead:
                    wait_alone(sp, y1_stored, (b + 1) * (16 * NT))
                    sp.dma_start(z_tok[:, :, :], of_batch(x_v, b + 1)).then_inc(z_loaded, 16)

            with sp.Fori(0, B - 1) as b:
                batch(b, True)
            batch(B - 1, False)

            sp.wait_ge(y1_stored, 16 * B * NT)
            sp.dma_start(x_tok[:, :, :], y1_v[0]).then_inc(y_loaded, 16)
            sp.dma_start(z_tok[:, :, :], y1_v[0]).then_inc(r_loaded, 16)
            for r in range(FW_ROUNDS):
                if r >= 2:
                    sp.wait_ge(fw_shifted, (r - 1) * TPR)
                if r < NI // TPR:
                    src = gate_v[r]
                elif r < 2 * NI // TPR:
                    src = up_v[r - NI // TPR]
                else:
                    src = down_v[r - 2 * NI // TPR]
                sp.dma_start(w_int[:, r % 2, :, :], src).then_inc(fw_loaded[r % 2], 16)
            with nc.allow_non_contiguous_dma(reason="a scale per partition"):
                sp.dma_start(g_scale[:, :], gate_scale.rearrange("(c p) -> p c", p=P)).then_inc(scales_loaded, 16)
                sp.dma_start(u_scale[:, :], up_scale.rearrange("(c p) -> p c", p=P)).then_inc(scales_loaded, 16)
            sp.dma_start(d_scale[:, :], down_scale.partition_broadcast(P)).then_inc(scales_loaded, 16)

            def ffn_batch(b, ahead):
                if ahead:
                    wait_alone(sp, yT_full, (b + 1) * ND)
                    sp.dma_start(x_tok[:, :, :], of_batch(y1_v, b + 1)).then_inc(y_loaded, 16)
                for t in range(NT):
                    wait_alone(sp, out_done, b * NT + t + 1)
                    sp.dma_start(of_batch(out_v, b)[:, t, :], z_tok[:, t, :]).then_inc(out_stored, 16)
                if ahead:
                    wait_alone(sp, out_stored, (b + 1) * (16 * NT))
                    sp.dma_start(z_tok[:, :, :], of_batch(y1_v, b + 1)).then_inc(r_loaded, 16)

            with sp.Fori(0, B - 1) as b:
                ffn_batch(b, True)
            ffn_batch(B - 1, False)
            sp.wait_ge(out_stored, 16 * B * NT)

        @block.gpsimd
        def _(pool):
            nc.gpsimd.memset(ident[:, :], 0.0)
            nc.gpsimd.memset(causal[:, :], 0.0)
            nc.gpsimd.memset(ones[:, :], 1.0)
            nc.gpsimd.memset(half_power[:, :], -0.5).then_inc(pool_step, 1)
            pool.wait_ge(pool_step, 1)
            nc.gpsimd.affine_select(out=ident[:, :], in_=ident[:, :], compare_op=ALU.not_equal, fill=1.0, base=0,
                                    pattern=[[-1, P]], channel_multiplier=1)
            nc.gpsimd.affine_select(out=causal[:, S - P:S], in_=causal[:, S - P:S], compare_op=ALU.is_ge, fill=FLOOR,
                                    base=0, pattern=[[-1, P]], channel_multiplier=1).then_inc(consts_ready, 1)
            pool.wait_ge(bias_loaded, 16 * (HG + 2))

            def batch(b):
                for g in range(NG):
                    if g == NG // 2:
                        pool.wait_ge(z_loaded, b * 16 + 16)
                        for t in range(NT):
                            last = nc.gpsimd.tensor_tensor(z_tok[:, t, :], z_tok[:, t, :], bias_o[:, :], ALU.add)
                        last.then_inc(res_ready, 1)
                    for kb in range(NT):
                        wait_alone(pool, exp_done, (b * NG + g) * SLOTS + HG * (kb + 1))
                        tri = probs[kb][:, :, 0:P]
                        nc.gpsimd.affine_select(out=tri, in_=tri, compare_op=ALU.is_ge, fill=0.0, base=0,
                                                pattern=[[0, HG], [1, P]],
                                                channel_multiplier=-1).then_inc(probs_masked, 1)
                pool.wait_ge(var_done, b + 1)
                nc.gpsimd.tensor_tensor(ln_rstd[:, :], ln_var[:, :], half_power[:, :], ALU.pow).then_inc(rstd_done, 1)

            with pool.Fori(0, B) as b:
                batch(b)
            with pool.Fori(0, B) as b:
                pool.wait_ge(var2_done, b + 1)
                nc.gpsimd.tensor_tensor(ln_rstd[:, :], ln_var[:, :], half_power[:, :], ALU.pow).then_inc(rstd2_done, 1)

        @block.scalar
        def _(act):
            with act.Fori(0, NROUND // 2) as r:
                for s in range(TPR):
                    act.wait_ge(w_full, r * TPR + s + 1)
                    nc.scalar.activation(by_row(wT_hi, r * (TPR * P) + s * P),
                                         pj[s % 2][:, :].rearrange("p (c j d) -> p c j d", c=ND, j=HG),
                                         ACT.Copy).then_inc(w_hi_done, 1)
            with act.Fori(NROUND // 2, NROUND) as r:
                for s in range(TPR):
                    act.wait_ge(w_full, r * TPR + s + 1)
                    nc.scalar.activation(wT_hi[:, :, bass.ds(r * (TPR * P) + s * P, P)],
                                         pj[s % 2][:, :].rearrange("p (c e) -> p c e", c=ND),
                                         ACT.Copy).then_inc(w_hi_done, 1)
            act.wait_ge(bias_loaded, 16 * (HG + 2))

            def x_hi(jobs, c):
                act.wait_ge(pj_full[jobs.bank("x", c)], jobs.done("x", c))
                nc.scalar.activation(xT_hi[:, c, :], pj[jobs.bank("x", c)][:, :], ACT.Copy).then_inc(x_hi_done, 1)

            def qk_hi(jobs, b, kind, r):
                n = "qk".index(kind)
                act.wait_ge(pj_full[jobs.bank(kind, r)], jobs.done(kind, r))
                if r >= 1:
                    act.wait_ge(stacked, (b * NG + r) * STACK_DMAS)
                chunk = n * NG + r % NG
                nc.scalar.activation((q_hi, k_hi)[n][:, :], pj[jobs.bank(kind, r)][:, :], ACT.Identity,
                                     bias=bias_qk[:, chunk:chunk + 1]).then_inc(qk_hi_done, 1)

            def inverse_estimate(b, g):
                act.wait_ge(pv_full, b * NG + g + 1)
                nc.scalar.activation(log_sum[:, :], sum_acc[:, :], ACT.Ln).then_inc(log_done, 1)
                act.wait_ge(log_done, b * NG + g + 1)
                nc.scalar.activation(inv_est[:, :], log_sum[:, :], ACT.Exp, scale=-1.0).then_inc(est_done, 1)

            def att_hi(b, g):
                act.wait_ge(att_done, b * NG + g + 2)
                nc.scalar.activation(attT_hi[:, g, :], attT[:, :], ACT.Copy).then_inc(att_hi_done, 1)

            for c in range(ND):
                x_hi(front_jobs, c)
            for r in range(2):
                for kind in "qk":
                    qk_hi(front_jobs, 0, kind, r)

            def batch(b, ahead):
                jobs = jobs_of(b, ahead)
                for g in range(NG):
                    for s in range(SLOTS):
                        kb, j = divmod(s, HG)
                        act.wait_ge(scoreT_full, (b * NG + g) * SLOTS + s + 1)
                        nc.scalar.activation(probs[kb][:, j, :], scoreT[s % 2][:, 0:P_WIDTH[kb]], ACT.Exp,
                                             scale=SCALE).then_inc(exp_done, 1)
                        if ahead and g == NG - 2 and s < 2:
                            x_hi(jobs, 2 + s)
                        if ahead and g == NG - 3 and s == SLOTS - 1:
                            x_hi(jobs, 0)
                            x_hi(jobs, 1)
                        if g > 0 and s == 3:
                            inverse_estimate(b, g - 1)
                        if g > 0 and s == 7:
                            att_hi(b, g - 1)
                        if ("q", g + 2) in jobs.place and s == 8:
                            qk_hi(jobs, b, "q", g + 2)
                        if ("k", g + 2) in jobs.place and s == 14:
                            qk_hi(jobs, b, "k", g + 2)
                inverse_estimate(b, NG - 1)
                att_hi(b, NG - 1)

            with act.Fori(0, B - 1) as b:
                batch(b, True)
            batch(B - 1, False)

            def y_hi(b, c):
                act.wait_ge(yT_full, b * ND + c + 1)
                nc.scalar.activation(xT_hi[:, c, :], y_bank[c][:, :], ACT.Copy).then_inc(yT_hi_done, 1)

            for n in range(0, NFW, 2):
                evict_ffn_weight(act, n, lambda o, i: nc.scalar.activation(o, i, ACT.Copy))
            act.wait_ge(scales_loaded, 48)
            for c in range(ND):
                y_hi(0, c)

            def ffn_batch(b, ahead):
                for i in range(NI):
                    act.wait_ge(gate_full, b * NI + i + 1)
                    nc.scalar.activation(silu[:, i % 2, :], gate_acc[i % 2][:, :], ACT.Silu,
                                         scale=g_scale[:, i:i + 1]).then_inc(silu_done, 1)
                    act.wait_ge(hid_done, b * NI + i + 1)
                    if i >= 2:
                        act.wait_ge(down_full, b * NI + i - 1)
                    nc.scalar.activation(hid_hi[:, i % 2, :], hid[:, i % 2, :], ACT.Copy).then_inc(hid_hi_done, 1)
                if ahead:
                    for c in range(ND):
                        y_hi(b + 1, c)

            with act.Fori(0, B - 1) as b:
                ffn_batch(b, True)
            ffn_batch(B - 1, False)

        @block.vector
        def _(dve):
            for i in range(2):
                nc.vector.memset(k_stack[i][STAT:P, :, :].bitcast(F32), 1.0)
                last = nc.vector.memset(q_stack[i][STAT:P, :, :].bitcast(F32), 0.0)
            last.then_inc(stacks_set, 1)
            nc.vector.memset(ln_var[:, :], 1.0).then_inc(att_done, 1)
            nc.vector.memset(ln_mv[:, :, :], 0.0).then_inc(d_done, 1)
            with dve.Fori(0, NROUND // 2) as r:
                for s in range(TPR):
                    first = r * (TPR * P) + s * P
                    dve.wait_ge(w_hi_done, r * TPR + s + 1)
                    nc.vector.tensor_tensor(by_row(wT_lo, first),
                                            pj[s % 2][:, :].rearrange("p (c j d) -> p c j d", c=ND, j=HG),
                                            by_row(wT_hi, first).bitcast(F32), ALU.subtract).then_inc(w_free, 1)
            with dve.Fori(NROUND // 2, NROUND) as r:
                for s in range(TPR):
                    col = bass.ds(r * (TPR * P) + s * P, P)
                    dve.wait_ge(w_hi_done, r * TPR + s + 1)
                    nc.vector.tensor_tensor(wT_lo[:, :, col], pj[s % 2][:, :].rearrange("p (c e) -> p c e", c=ND),
                                            wT_hi[:, :, col].bitcast(F32), ALU.subtract).then_inc(w_free, 1)
            dve.wait_ge(bias_loaded, 16 * (HG + 2))
            dve.wait_ge(consts_ready, 1)

            def x_lo(jobs, count, c):
                dve.wait_ge(x_hi_done, count + c + 1)
                nc.vector.tensor_tensor(xT_lo[:, c, :], pj[jobs.bank("x", c)][:, :], xT_hi[:, c, :].bitcast(F32),
                                        ALU.subtract).then_inc(pj_drained[jobs.bank("x", c)], 1)

            def qk_lo(jobs, b, kind, r):
                n = "qk".index(kind)
                chunk = n * NG + r % NG
                dve.wait_ge(qk_hi_done, (b * NG + r) * 2 + n + 1)
                nc.vector.scalar_tensor_tensor(
                    out=(q_lo, k_lo)[n][:, :], in0=pj[jobs.bank(kind, r)][:, :], scalar=bias_qk[:, chunk:chunk + 1],
                    in1=(q_hi, k_hi)[n][:, :].bitcast(F32), op0=ALU.add,
                    op1=ALU.subtract).then_inc(pj_drained[jobs.bank(kind, r)], 1)

            def values(jobs, t):
                dve.wait_ge(pj_full[jobs.bank("v", t)], jobs.done("v", t))
                nc.vector.tensor_tensor(v_tok[:, t, :], pj[jobs.bank("v", t)][:, :], bias_v[:, :],
                                        ALU.add).then_inc(pj_drained[jobs.bank("v", t)], 1)

            def tile_max(b, r, s):
                j, qb = divmod(s, NT)
                w = (qb + 1) * P
                wait_alone(dve, score_full, (b * NG + r) * SLOTS + s + 1)
                nc.vector.tensor_tensor_reduce(
                    out=masked[:, s % 2, 0:w], in0=score[s % 2][:, 0:w], in1=causal[:, S - w:S], scale=1.0, scalar=FLOOR,
                    op0=ALU.add, op1=ALU.max, accum_out=row_max[:, qb, j:j + 1]).then_inc(max_done, 1)

            def split_max(b, r):
                dve.wait_ge(max_done, (b * NG + r + 1) * SLOTS)
                nc.vector.tensor_scalar(neg_max[:, :, 0, :], row_max[:, :, :], -1.0, None, ALU.mult).then_inc(max_hi_done, 1)
                dve.wait_ge(max_hi_done, b * NG + r + 1)
                nc.vector.scalar_tensor_tensor(out=neg_max[:, :, 1, :], in0=row_max[:, :, :], scalar=-1.0,
                                               in1=neg_max[:, :, 0, :].bitcast(F32), op0=ALU.mult,
                                               op1=ALU.subtract).then_inc(max_split, 1)

            def keep_max_rows(jobs, b, r):
                dve.wait_ge(pj_full[jobs.bank("m", r)], jobs.done("m", r))
                if r >= 1:
                    dve.wait_ge(max_placed, (b * NG + r) * 16)
                nc.vector.tensor_copy(max_rows[:, :],
                                      pj[jobs.bank("m", r)][0:2 * HG, :]).then_inc(pj_drained[jobs.bank("m", r)], 1)

            def normalise(b, g):
                n = b * NG + g + 1
                dve.wait_ge(est_done, n)
                nc.vector.tensor_tensor(inv_err[:, :], sum_acc[:, :], inv_est[:, :], ALU.mult).then_inc(err_done, 1)
                dve.wait_ge(err_done, n)
                nc.vector.scalar_tensor_tensor(out=neg_inv[:, :], in0=inv_err[:, :], scalar=-2.0, in1=inv_est[:, :],
                                               op0=ALU.add, op1=ALU.mult).then_inc(inv_done, 1)
                dve.wait_ge(inv_done, n)
                nc.vector.scalar_tensor_tensor(out=attT[:, :], in0=pv_acc[:, :], scalar=-1.0, in1=neg_inv[:, :],
                                               op0=ALU.mult, op1=ALU.mult).then_inc(att_done, 1)

            def att_lo(b, g):
                dve.wait_ge(att_hi_done, b * NG + g + 1)
                nc.vector.tensor_tensor(attT_lo[:, g, :], attT[:, :], attT_hi[:, g, :].bitcast(F32),
                                        ALU.subtract).then_inc(att_ready, 1)

            def statistics(b, t, stat, mv):
                nc.vector.bn_stats(ln_stat[:, t, :], z_tok[:, t, :]).then_inc(stat, 1)
                wait_alone(dve, stat, b * NT + t + 1)
                nc.vector.bn_aggr(ln_mv[:, t, :], ln_stat[:, t, :]).then_inc(mv, 1)

            def layer_norm(b, mv, var, rstd, done):
                dve.wait_ge(mv, (b + 1) * NT)
                nc.vector.tensor_scalar(ln_var[:, :], ln_mv[:, :, 1], EPS, None, ALU.add).then_inc(var, 1)
                dve.wait_ge(rstd, b + 1)
                for t in range(NT):
                    nc.vector.tensor_scalar(z_tok[:, t, :], z_tok[:, t, :], ln_mv[:, t, 0:1], ln_rstd[:, t:t + 1],
                                            ALU.subtract, ALU.mult).then_inc(done, 1)

            for c in range(ND):
                x_lo(front_jobs, 0, c)
            for kind in "qk":
                qk_lo(front_jobs, 0, kind, 0)
            for t in range(NT):
                values(front_jobs, t)
            for s in range(SLOTS):
                tile_max(0, 0, s)
                if s == 7:
                    qk_lo(front_jobs, 0, "q", 1)
                if s == 13:
                    qk_lo(front_jobs, 0, "k", 1)
            split_max(0, 0)
            keep_max_rows(front_jobs, 0, 0)

            def batch(b, ahead):
                jobs = jobs_of(b, ahead)
                for g in range(NG):
                    for s in range(SLOTS):
                        if ahead and g == NG - 2 and s in (1, 2):
                            x_lo(jobs, (b + 1) * ND, 1 + s)
                        if ("m", g + 1) in jobs.place and 2 <= s < 10:
                            tile_max(b, g + 1, 2 * (s - 2))
                            tile_max(b, g + 1, 2 * (s - 2) + 1)
                        if g > 0 and s == 4:
                            normalise(b, g - 1)
                        if g > 0 and s == 7:
                            att_lo(b, g - 1)
                        if ("q", g + 2) in jobs.place and s == 8:
                            qk_lo(jobs, b, "q", g + 2)
                        if ("m", g + 1) in jobs.place and s == 10:
                            split_max(b, g + 1)
                        if ("m", g + 1) in jobs.place and s == 12:
                            keep_max_rows(jobs, b, g + 1)
                        if ("k", g + 2) in jobs.place and s == 14:
                            qk_lo(jobs, b, "k", g + 2)
                    if ahead and g == NG - 3:
                        x_lo(jobs, (b + 1) * ND, 0)
                        x_lo(jobs, (b + 1) * ND, 1)
                normalise(b, NG - 1)
                att_lo(b, NG - 1)
                if ahead:
                    for t in range(NT):
                        values(jobs, t)
                dve.wait_ge(res_ready, b + 1)
                for t in range(NT):
                    dve.wait_ge(pj_full[jobs.bank("o", t)], jobs.done("o", t))
                    nc.vector.tensor_tensor(z_tok[:, t, :], pj[jobs.bank("o", t)][:, :], z_tok[:, t, :],
                                            ALU.add).then_inc(pj_drained[jobs.bank("o", t)], 1)
                    dve.wait_ge(pj_drained[jobs.bank("o", t)], jobs.done("o", t))
                    statistics(b, t, stat_done, mv_done)
                layer_norm(b, mv_done, var_done, rstd_done, y1_done)

            with dve.Fori(0, B - 1) as b:
                batch(b, True)
            batch(B - 1, False)

            for n in range(NFW):
                shift_ffn_weight(dve, n)
                if n >= 2 and (n - 2) % 2 == 1:
                    evict_ffn_weight(dve, n - 2, nc.vector.tensor_copy)
            evict_ffn_weight(dve, NFW - 1, nc.vector.tensor_copy)
            dve.wait_ge(scales_loaded, 48)

            def y_lo(b, c):
                dve.wait_ge(yT_hi_done, b * ND + c + 1)
                nc.vector.tensor_tensor(xT_lo[:, c, :], y_bank[c][:, :], xT_hi[:, c, :].bitcast(F32),
                                        ALU.subtract).then_inc(yT_done, 1)

            for c in range(ND):
                y_lo(0, c)

            def ffn_batch(b, ahead):
                for i in range(NI):
                    dve.wait_ge(up_full, b * NI + i + 1)
                    dve.wait_ge(silu_done, b * NI + i + 1)
                    nc.vector.scalar_tensor_tensor(out=hid[:, i % 2, :], in0=up_acc[i % 2][:, :],
                                                   scalar=u_scale[:, i:i + 1], in1=silu[:, i % 2, :], op0=ALU.mult,
                                                   op1=ALU.mult).then_inc(hid_done, 1)
                    dve.wait_ge(hid_hi_done, b * NI + i + 1)
                    nc.vector.tensor_tensor(hid_lo[:, i % 2, :], hid[:, i % 2, :], hid_hi[:, i % 2, :].bitcast(F32),
                                            ALU.subtract).then_inc(hid_ready, 1)
                if ahead:
                    for c in range(ND):
                        y_lo(b + 1, c)
                dve.wait_ge(r_loaded, b * 16 + 16)
                dve.wait_ge(down_full, (b + 1) * NI)
                for t in range(NT):
                    nc.vector.tensor_tensor(d_scaled[:, t % 2, :], down_acc[t][:, :], d_scale[:, :],
                                            ALU.mult).then_inc(d_done, 1)
                    dve.wait_ge(d_done, b * NT + t + 2)
                    nc.vector.tensor_tensor(z_tok[:, t, :], d_scaled[:, t % 2, :], z_tok[:, t, :],
                                            ALU.add).then_inc(z2_done, 1)
                    dve.wait_ge(z2_done, b * NT + t + 1)
                    statistics(b, t, stat2_done, mv2_done)
                layer_norm(b, mv2_done, var2_done, rstd2_done, out_done)

            with dve.Fori(0, B - 1) as b:
                ffn_batch(b, True)
            ffn_batch(B - 1, False)

        def split_product(acc, a_hi, a_lo, b_hi, b_lo, first, last):
            nc.tensor.matmul(acc, a_hi, b_hi, start=first, stop=False)
            nc.tensor.matmul(acc, a_hi, b_lo, start=False, stop=False)
            return nc.tensor.matmul(acc, a_lo, b_hi, start=False, stop=last)

        @block.tensor
        def _(pe):
            pe.wait_ge(consts_ready, 1)
            for r in range(NROUND):
                pe.wait_ge(w_loaded[r], 16)
                for s in range(TPR):
                    n = r * TPR + s
                    if n >= 2:
                        pe.wait_ge(w_free, n - 1)
                    for c in range(ND):
                        last = nc.tensor.transpose(pj[n % 2][:, c * P:(c + 1) * P], w_stage[r % 3][:, s, c * P:(c + 1) * P],
                                                   ident[:, :])
                    last.then_inc(w_full, 1)
            pe.wait_ge(w_free, NROUND * TPR)
            pe.wait_ge(stacks_set, 1)

            def bank_for(jobs, *job):
                if jobs.before_it(*job) is not None:
                    pe.wait_ge(pj_drained[jobs.bank(*job)], jobs.before_it(*job))
                return pj[jobs.bank(*job)]

            def transpose_x(jobs, b, c):
                if c == 0:
                    pe.wait_ge(x_loaded, b * 16 + 16)
                acc = bank_for(jobs, "x", c)
                for t in range(NT):
                    last = nc.tensor.transpose(acc[:, t * P:(t + 1) * P], x_tok[:, t, c * P:(c + 1) * P], ident[:, :])
                last.then_inc(pj_full[jobs.bank("x", c)], 1)

            def project(jobs, x_jobs, r):
                for n, kind in enumerate("qk"):
                    acc = bank_for(jobs, kind, r)
                    e = slice(n * D + r % NG * P, n * D + (r % NG + 1) * P)
                    for c in range(ND):
                        if x_jobs is not None and n == 0:
                            pe.wait_ge(pj_drained[x_jobs.bank("x", c)], x_jobs.done("x", c))
                        first, final = c == 0, c == ND - 1
                        nc.tensor.matmul(acc[:, :], wT_hi[:, c, e], xT_hi[:, c, :], start=first, stop=False)
                        yield
                        nc.tensor.matmul(acc[:, :], wT_hi[:, c, e], xT_lo[:, c, :], start=False, stop=False)
                        yield
                        last = nc.tensor.matmul(acc[:, :], wT_lo[:, c, e], xT_hi[:, c, :], start=False, stop=final)
                        if final:
                            last.then_inc(pj_full[jobs.bank(kind, r)], 1)
                        yield

            def project_values(jobs, t):
                acc = bank_for(jobs, "v", t)
                tok = slice(t * P, (t + 1) * P)
                for c in range(ND):
                    last = split_product(acc[:, :], xT_hi[:, c, tok], xT_lo[:, c, tok], wT_hi[:, c, 2 * D:3 * D],
                                         wT_lo[:, c, 2 * D:3 * D], c == 0, c == ND - 1)
                last.then_inc(pj_full[jobs.bank("v", t)], 1)

            def scores(b, r, s):
                j, qb = divmod(s, NT)
                w = (qb + 1) * P
                if s == 0:
                    pe.wait_ge(stacked, (b * NG + r + 1) * STACK_DMAS)
                if r > 0 or s >= 2:
                    pe.wait_ge(max_done, (b * NG + r) * SLOTS + s - 1)
                nc.tensor.matmul(score[s % 2][:, 0:w], q_stack[r % 2][0:STAT, j, qb * P:(qb + 1) * P],
                                 k_stack[r % 2][0:STAT, j, 0:w], start=True, stop=True).then_inc(score_full, 1)

            def scores_transposed(b, g, s):
                kb, j = divmod(s, HG)
                if s == 0:
                    pe.wait_ge(max_placed, (b * NG + g + 1) * 16)
                if g > 0 or s >= 2:
                    pe.wait_ge(exp_done, (b * NG + g) * SLOTS + s - 1)
                nc.tensor.matmul(scoreT[s % 2][:, 0:P_WIDTH[kb]], k_stack[g % 2][:, j, kb * P:(kb + 1) * P],
                                 q_stack[g % 2][:, j, kb * P:S], start=True, stop=True).then_inc(scoreT_full, 1)

            def weighted_values(b, g, kb):
                if kb == 0:
                    pe.wait_ge(att_done, b * NG + g + 1)
                pe.wait_ge(probs_masked, (b * NG + g) * NT + kb + 1)
                for j in range(HG):
                    h = g * HG + j
                    nc.tensor.matmul(pv_acc[j * HD:(j + 1) * HD, kb * P:S], v_tok[:, kb, h * HD:(h + 1) * HD],
                                     probs[kb][:, j, :], start=kb == 0, stop=kb == NT - 1)
                for j in range(HG):
                    last = nc.tensor.matmul(sum_acc[j * HD:(j + 1) * HD, kb * P:S], ones[:, :], probs[kb][:, j, :],
                                            start=kb == 0, stop=kb == NT - 1)
                if kb == NT - 1:
                    last.then_inc(pv_full, 1)

            def max_to_rows(jobs, b, r):
                acc = bank_for(jobs, "m", r)
                pe.wait_ge(max_split, b * NG + r + 1)
                for qb in range(NT):
                    last = nc.tensor.transpose(acc[0:2 * HG, qb * P:(qb + 1) * P],
                                               neg_max[:, qb, :, :].bitcast(F32).rearrange("p n j -> p (n j)"),
                                               ident[:, :])
                last.then_inc(pj_full[jobs.bank("m", r)], 1)

            for c in range(ND):
                transpose_x(front_jobs, 0, c)
            for _ in project(front_jobs, front_jobs, 0):
                pass
            for t in range(NT):
                project_values(front_jobs, t)
            work = project(front_jobs, None, 1)
            for s in range(SLOTS):
                scores(0, 0, s)
                if s < 12:
                    next(work)
                    next(work)
            next(work, None)
            max_to_rows(front_jobs, 0, 0)

            def batch(b, ahead):
                jobs = jobs_of(b, ahead)
                for g in range(NG):
                    if ("q", g + 2) in jobs.place:
                        work = project(jobs, jobs if g + 2 == NG else None, g + 2)
                    for s in range(SLOTS):
                        if ahead and g == NG - 2 and s < 2:
                            transpose_x(jobs, b + 1, 2 + s)
                        if ("m", g + 1) in jobs.place and 2 <= s < 10:
                            scores(b, g + 1, 2 * (s - 2))
                            scores(b, g + 1, 2 * (s - 2) + 1)
                        scores_transposed(b, g, s)
                        if g > 0 and s == 1:
                            weighted_values(b, g - 1, NT - 1)
                        if s in (6, 10, 14):
                            weighted_values(b, g, (s - 6) // 4)
                        if ("q", g + 2) in jobs.place and 2 <= s < 14:
                            next(work)
                            next(work)
                        if ("m", g + 1) in jobs.place and s == 12:
                            max_to_rows(jobs, b, g + 1)
                        if ahead and g == NG - 3 and s >= SLOTS - 2:
                            if s == SLOTS - 2:
                                next(work, None)
                            transpose_x(jobs, b + 1, s - (SLOTS - 2))
                    if ("q", g + 2) in jobs.place:
                        next(work, None)
                weighted_values(b, NG - 1, NT - 1)
                if ahead:
                    for t in range(NT):
                        project_values(jobs, t)
                pe.wait_ge(att_ready, (b + 1) * NG)
                for t in range(NT):
                    acc = bank_for(jobs, "o", t)
                    tok = slice(t * P, (t + 1) * P)
                    for c in range(NG):
                        last = split_product(acc[:, :], attT_hi[:, c, tok], attT_lo[:, c, tok], wT_hi[:, c, NE:NE + D],
                                             wT_lo[:, c, NE:NE + D], c == 0, c == NG - 1)
                    last.then_inc(pj_full[jobs.bank("o", t)], 1)

            with pe.Fori(0, B - 1) as b:
                batch(b, True)
            batch(B - 1, False)

            last_jobs = jobs_of(B - 1, False)
            for n in range(NFW):
                pe.wait_ge(fw_shifted, n + 1)
                if n >= 2:
                    pe.wait_ge(fw_free[n % 2], n // 2)
                else:
                    t = NT - 2 + n
                    pe.wait_ge(pj_drained[last_jobs.bank("o", t)], last_jobs.done("o", t))
                for c in range(TPR):
                    last = nc.tensor.transpose(pj[n % 2][:, c * P:(c + 1) * P], w_shift[:, n % 2, c * P:(c + 1) * P],
                                               ident[:, :])
                last.then_inc(fw_full, 1)
            for i in range(2):
                pe.wait_ge(fw_free[i], NFW // 2)

            def transpose_y(b, c):
                if c == 0:
                    pe.wait_ge(y_loaded, b * 16 + 16)
                for t in range(NT):
                    last = nc.tensor.transpose(y_bank[c][:, t * P:(t + 1) * P], x_tok[:, t, c * P:(c + 1) * P], ident[:, :])
                last.then_inc(yT_full, 1)

            for c in range(ND):
                transpose_y(0, c)

            def ffn_batch(b, ahead):
                def gate_up(i):
                    cols = slice(i * P, (i + 1) * P)
                    if i >= 2:
                        pe.wait_ge(hid_done, b * NI + i - 1)
                    for w, acc, full in ((gateT, gate_acc, gate_full), (upT, up_acc, up_full)):
                        for c in range(ND):
                            if i == 0 and w is gateT:
                                pe.wait_ge(yT_done, b * ND + (c + 1 if c else 1))
                            nc.tensor.matmul(acc[i % 2][:, :], w[:, c, cols], xT_hi[:, c, :], start=c == 0, stop=False)
                            last = nc.tensor.matmul(acc[i % 2][:, :], w[:, c, cols], xT_lo[:, c, :], start=False,
                                                    stop=c == ND - 1)
                        last.then_inc(full, 1)

                def down(i):
                    pe.wait_ge(hid_ready, b * NI + i + 1)
                    if i == 0:
                        pe.wait_ge(d_done, b * NT + 1)
                    for t in range(NT):
                        tok = slice(t * P, (t + 1) * P)
                        nc.tensor.matmul(down_acc[t][:, :], hid_hi[:, i % 2, tok], downT[:, i, :], start=i == 0, stop=False)
                        last = nc.tensor.matmul(down_acc[t][:, :], hid_lo[:, i % 2, tok], downT[:, i, :], start=False,
                                                stop=i == NI - 1)
                    last.then_inc(down_full, 1)

                gate_up(0)
                for i in range(1, NI):
                    gate_up(i)
                    down(i - 1)
                if ahead:
                    pe.wait_ge(hid_done, b * NI + NI - 1)
                    transpose_y(b + 1, 0)
                    transpose_y(b + 1, 1)
                down(NI - 1)
                if ahead:
                    pe.wait_ge(hid_done, b * NI + NI)
                    transpose_y(b + 1, 2)
                    transpose_y(b + 1, 3)

            with pe.Fori(0, B - 1) as b:
                ffn_batch(b, True)
            ffn_batch(B - 1, False)


_INS = ['L0_attn_x', 'L0_attn_w_qkv', 'L0_attn_b_qkv', 'L0_attn_w_out', 'L0_attn_b_out', 'L0_ffn_gate_w',
        'L0_ffn_gate_scale', 'L0_ffn_up_w', 'L0_ffn_up_scale', 'L0_ffn_down_w', 'L0_ffn_down_scale']


def kernel(**inputs):
    import numpy as _np
    import concourse.bacc as _bacc
    from concourse import mybir as _mybir
    from concourse.bass_utils import run_bass_kernel_spmd as _run

    nc = _bacc.Bacc("TRN2", target_bir_lowering=False, num_devices=1)
    arrays, args = {}, []
    for name in _INS:
        a = _np.ascontiguousarray(inputs[name])
        arrays[f"in_{name}_dram"] = a
        args.append(nc.dram_tensor(f"in_{name}_dram", a.shape, _mybir.dt.from_np(a.dtype), kind="ExternalInput").ap())
    shape = inputs['L0_attn_x'].shape
    args.append(nc.dram_tensor("out_0_dram", shape, _mybir.dt.float32, kind="ExternalOutput").ap())
    postln_block_kernel(nc, *args)
    r = _run(nc, [arrays], core_ids=[0])
    return r.results[0]["out_0_dram"]
```

```python
import concourse.bass as bass
from concourse import mybir
from contextlib import ExitStack


def postln_block_kernel(nc: bass.Bass, x, w_qkv, b_qkv, w_out, b_out, gate_w, gate_scale, up_w, up_scale,
                        down_w, down_scale, out):
    F32, F32R, I32 = mybir.dt.float32, mybir.dt.float32r, mybir.dt.int32
    ALU, ACT = mybir.AluOpType, mybir.ActivationFunctionType

    P = 128
    B, S, D = x.shape
    HD = 32
    H = D // HD
    I = gate_w.shape[0]
    ND = D // P
    NT = S // P
    NI = I // P
    HG = P // HD
    NG = H // HG
    NE = 3 * D
    UNITS = NG * NT
    BLOCKS = NT * (NT + 1) // 2
    AHEAD = 2
    SCALE = float(HD) ** -0.5
    EPS = 1e-5
    ZERO_POINT = 128.0
    FLOOR = -3.0e38
    TPR = 4
    NROUND = (NE + D) // (P * TPR)
    STACK = 3 * HD
    STACK_DMAS = 6 * 16

    FRONT = ([("x", c) for c in range(ND)] + [("q", 0), ("k", 0)] + [("v", t) for t in range(NT)] +
             [("q", 1), ("k", 1)])

    def batch_jobs(ahead):
        jobs = []
        for g in range(NG):
            if ahead or g + 2 < NG:
                jobs += [("q", g + 2), ("k", g + 2)]
            jobs += [("r", g)]
            if ahead and g == NG - 3:
                jobs += [("x", c) for c in range(ND)]
        return jobs + [("v", t) for t in range(NT) if ahead] + [("o", t) for t in range(NT)]

    PER_BATCH = len(batch_jobs(True))
    assert PER_BATCH % 2 == 0

    class Jobs:

        def __init__(self, b, jobs, before):
            self.b, self.before = b, before
            self.place = {job: before + n for n, job in enumerate(jobs)}

        def bank(self, *job):
            return self.place[job] % 2

        def done(self, *job):
            return self.b * (PER_BATCH // 2) + self.place[job] // 2 + 1

        def before_it(self, *job):
            return None if self.place[job] < 2 else self.done(*job) - 1

    front_jobs = Jobs(0, FRONT, 0)

    def jobs_of(b, ahead):
        return Jobs(b, batch_jobs(ahead), len(FRONT))

    y1_dram = nc.dram_tensor("y1_scratch", (B * S, D), F32, kind="Internal").ap()
    x_v = x.rearrange("b (t p) d -> b p t d", p=P)
    y1_v = y1_dram.rearrange("(b t p) d -> b p t d", p=P, t=NT)
    out_v = out.rearrange("b (t p) d -> b p t d", p=P)
    gate_v = gate_w.rearrange("(r s p) d -> r p s d", p=P, s=TPR)
    up_v = up_w.rearrange("(r s p) d -> r p s d", p=P, s=TPR)
    down_v = down_w.rearrange("(t p) (s c) -> t p s c", p=P, c=D)

    def of_batch(view, b):
        return view[bass.ds(b, 1)].rearrange("o p t d -> (o p) t d")

    ctx = ExitStack()
    with ctx:
        def sb(name, shape, dt=F32, where=ctx):
            return where.enter_context(nc.sbuf_tensor(name, shape, dt))

        def sem(name):
            return ctx.enter_context(nc.semaphore(name))

        def sem_pair(name):
            return [sem(f"{name}{i}") for i in range(2)]

        ident = sb("ident", [P, P])
        x_tok = sb("x_tok", [P, NT, D])
        xT_hi = sb("xT_hi", [P, ND, S], F32R)
        xT_lo = sb("xT_lo", [P, ND, S], F32R)
        z_tok = sb("z_tok", [P, NT, D])
        ln_stat = sb("ln_stat", [P, NT, 6])
        ln_mv = sb("ln_mv", [P, NT, 2])
        ln_var = sb("ln_var", [P, NT])
        ln_rstd = sb("ln_rstd", [P, NT])
        half_power = sb("half_power", [P, NT])

        att = ExitStack()
        wT_hi = sb("wT_hi", [P, ND, NE + D], F32R, att)
        wT_lo = sb("wT_lo", [P, ND, NE + D], F32R, att)
        q_stack = [sb(f"q_stack{i}", [STACK, HG, S], F32R, att) for i in range(2)]
        k_stack = [sb(f"k_stack{i}", [STACK, HG, S], F32R, att) for i in range(2)]
        q_hi = sb("q_hi", [P, S], F32R, att)
        q_lo = sb("q_lo", [P, S], F32R, att)
        k_hi = sb("k_hi", [P, S], F32R, att)
        k_lo = sb("k_lo", [P, S], F32R, att)
        v_tok = sb("v_tok", [P, NT, D], F32, att)
        attT_hi = sb("attT_hi", [P, NG, S], F32R, att)
        attT_lo = sb("attT_lo", [P, NG, S], F32R, att)
        causal = sb("causal", [P, S], F32, att)
        row_max = sb("row_max", [P, NT, HG], F32, att)
        neg_max = sb("neg_max", [P, NT, HG], F32, att)
        row_sum = sb("row_sum", [P, NT, HG], F32, att)
        inv_sum = sb("inv_sum", [P, NT, HG], F32, att)
        inv_wide = sb("inv_wide", [P, 2, NT, HG, HD], F32, att)
        invT = sb("invT", [P, S], F32, att)
        attT = sb("attT", [P, 2, S], F32, att)
        bias_qk = sb("bias_qk", [P, 2 * NG], F32, att)
        bias_v = sb("bias_v", [P, D], F32, att)
        bias_o = sb("bias_o", [P, D], F32, att)
        P_WIDTH = [(qb + 1) * P for qb in range(NT)]
        P_FIRST = [HG * sum(P_WIDTH[:qb]) for qb in range(NT)]
        probs_sb = sb("probs_sb", [P, HG * sum(P_WIDTH)], F32, att)
        probs = [probs_sb[:, P_FIRST[qb]:P_FIRST[qb] + HG * P_WIDTH[qb]].rearrange("p (j k) -> p j k", j=HG)
                 for qb in range(NT)]
        probsT = sb("probsT", [P, 4, HG, P], F32, att)
        w_stage = [t.rearrange("p (s d) -> p s d", s=TPR) for t in
                   (probs_sb[:, 0:TPR * D], probs_sb[:, TPR * D:2 * TPR * D])] + [z_tok[:, :, :]]
        att.close()

        ffn = ExitStack()
        gateT = sb("gateT", [P, ND, I], F32R, ffn)
        upT = sb("upT", [P, ND, I], F32R, ffn)
        downT = sb("downT", [P, NI, D], F32R, ffn)
        w_int = sb("w_int", [P, 2, TPR, D], I32, ffn)
        w_shift = sb("w_shift", [P, 2, D], F32, ffn)
        silu = sb("silu", [P, 2, S], F32, ffn)
        hid = sb("hid", [P, 2, S], F32, ffn)
        hid_hi = sb("hid_hi", [P, 2, S], F32R, ffn)
        hid_lo = sb("hid_lo", [P, 2, S], F32R, ffn)
        d_scaled = sb("d_scaled", [P, 2, D], F32, ffn)
        g_scale = sb("g_scale", [P, NI], F32, ffn)
        u_scale = sb("u_scale", [P, NI], F32, ffn)
        d_scale = sb("d_scale", [P, D], F32, ffn)
        ffn.close()

        bank = [ctx.enter_context(nc.psum_tensor(f"bank{i}", [P, 512], F32)) for i in range(8)]
        pj, score, pT, pv_acc = bank[0:2], bank[2:4], bank[4:6], bank[6:8]
        gate_acc, up_acc, down_acc = bank[0:2], bank[2:4], bank[4:8]
        y_bank = [gate_acc[0], up_acc[0], gate_acc[1], up_acc[1]]

        consts_ready = sem("consts_ready")
        pool_step = sem("pool_step")
        bias_loaded = sem("bias_loaded")
        w_loaded = [sem(f"w_loaded{r}") for r in range(NROUND)]
        w_full = sem("w_full")
        w_hi_done = sem("w_hi_done")
        w_free = sem("w_free")
        x_loaded = sem("x_loaded")
        z_loaded = sem("z_loaded")
        res_ready = sem("res_ready")
        pj_full = sem_pair("pj_full")
        pj_drained = sem_pair("pj_drained")
        x_hi_done = sem("x_hi_done")
        qk_hi_done = sem("qk_hi_done")
        stacked = sem("stacked")
        score_full = sem("score_full")
        max_done = sem("max_done")
        neg_done = sem("neg_done")
        exp_done = sem("exp_done")
        inv_done = sem("inv_done")
        inv_widened = sem("inv_widened")
        pT_full = sem("pT_full")
        pT_evicted = [sem("pT_evicted_act"), sem("pT_evicted_dve")]
        pv_full = sem("pv_full")
        att_done = sem("att_done")
        att_hi_done = sem("att_hi_done")
        att_ready = sem("att_ready")
        z_done = sem("z_done")
        stat_done = sem("stat_done")
        mv_done = sem("mv_done")
        var_done = sem("var_done")
        rstd_done = sem("rstd_done")
        y1_done = sem("y1_done")
        y1_stored = sem("y1_stored")
        scales_loaded = sem("scales_loaded")
        fw_loaded = sem_pair("fw_loaded")
        fw_shifted = sem("fw_shifted")
        fw_full = sem("fw_full")
        fw_free = [sem("fw_free_act"), sem("fw_free_dve")]
        y_loaded = sem("y_loaded")
        r_loaded = sem("r_loaded")
        yT_full = sem("yT_full")
        yT_hi_done = sem("yT_hi_done")
        yT_done = sem("yT_done")
        gate_full = sem("gate_full")
        up_full = sem("up_full")
        silu_done = sem("silu_done")
        hid_done = sem("hid_done")
        hid_hi_done = sem("hid_hi_done")
        hid_ready = sem("hid_ready")
        down_full = sem("down_full")
        d_done = sem("d_done")
        z2_done = sem("z2_done")
        stat2_done = sem("stat2_done")
        mv2_done = sem("mv2_done")
        var2_done = sem("var2_done")
        rstd2_done = sem("rstd2_done")
        out_done = sem("out_done")
        out_stored = sem("out_stored")

        NFW = 2 * NI + ND * NI // TPR
        FW_ROUNDS = NFW // TPR

        def wait_alone(eng, sem, value):
            value = eng.to_reg(value) if not isinstance(value, int) else value
            eng.wait_ge(consts_ready, 1)
            eng.wait_ge(sem, value)

        def ffn_weight_place(n):
            if n < NI:
                return gateT[:, :, n * P:(n + 1) * P]
            if n < 2 * NI:
                return upT[:, :, (n - NI) * P:(n - NI + 1) * P]
            t, s = divmod(n - 2 * NI, TPR)
            return downT[:, TPR * s:TPR * (s + 1), t * P:(t + 1) * P]

        def evict_ffn_weight(eng, n, copy):
            eng.wait_ge(fw_full, n + 1)
            copy(ffn_weight_place(n), pj[n % 2][:, :].rearrange("p (c e) -> p c e", c=TPR)).then_inc(fw_free[n % 2], 1)

        def shift_ffn_weight(dve, n):
            r, s = divmod(n, TPR)
            dve.wait_ge(fw_loaded[r % 2], 16 * (r // 2 + 1))
            if n >= 2:
                dve.wait_ge(fw_full, n - 1)
            nc.vector.tensor_scalar(w_shift[:, n % 2, :], w_int[:, r % 2, s, :], -ZERO_POINT, None,
                                    ALU.add).then_inc(fw_shifted, 1)

        def evict_block(eng, parity, b, n, copy):
            eng.wait_ge(pT_full, b * (NG * BLOCKS) + n + 1)
            copy(probsT[:, n % 4, :, :], pT[parity][:, :].rearrange("p (j q) -> p j q", j=HG)).then_inc(
                pT_evicted[parity], 1)

        def block_of(u, kb):
            g, qb = divmod(u, NT)
            return g * BLOCKS + qb * (qb + 1) // 2 + kb

        def by_row(wT, first):
            return wT[:, :, bass.ds(first, P)].rearrange("p c (d j) -> p c j d", j=HG)

        block = ctx.enter_context(nc.Block())

        @block.sync
        def _(sp):
            def load_w(r):
                src = w_qkv[r * TPR * P:(r + 1) * TPR * P, :] if r < NE // (TPR * P) else w_out
                sp.dma_start(w_stage[r % 3], src.rearrange("(s p) d -> p s d", p=P)).then_inc(w_loaded[r], 16)

            for r in range(3):
                load_w(r)
            sp.dma_start(x_tok[:, :, :], x_v[0]).then_inc(x_loaded, 16)
            with nc.allow_non_contiguous_dma(reason="a bias per partition"):
                for j in range(HG):
                    sp.dma_start(bias_qk[j:P:HG, :],
                                 b_qkv[0:2 * D].rearrange("(c j d) -> j d c", j=HG, d=HD)[j]).then_inc(bias_loaded, 16)
            sp.dma_start(bias_v[:, :], b_qkv[2 * D:3 * D].partition_broadcast(P)).then_inc(bias_loaded, 16)
            sp.dma_start(bias_o[:, :], b_out.partition_broadcast(P)).then_inc(bias_loaded, 16)
            sp.wait_ge(w_full, TPR)
            load_w(3)
            sp.wait_ge(w_full, 3 * TPR)
            sp.dma_start(z_tok[:, :, :], x_v[0]).then_inc(z_loaded, 16)

            def stack(jobs, b, r):
                wait_alone(sp, pj_drained[jobs.bank("k", r)], jobs.done("k", r))
                if r >= 2:
                    wait_alone(sp, score_full, b * (UNITS * HG) + (r - 1) * (NT * HG))
                for n, (qs, ks) in enumerate(((q_hi, k_hi), (q_hi, k_lo), (q_lo, k_hi))):
                    to = slice(HD * n, HD * (n + 1))
                    sp.dma_start(q_stack[r % 2][to, :, :].bitcast(F32), qs[:, :].bitcast(F32)).then_inc(stacked, 16)
                    sp.dma_start(k_stack[r % 2][to, :, :].bitcast(F32), ks[:, :].bitcast(F32)).then_inc(stacked, 16)

            stack(front_jobs, 0, 0)
            stack(front_jobs, 0, 1)

            def batch(b, ahead):
                jobs = jobs_of(b, ahead)
                if ahead:
                    sp.dma_start(x_tok[:, :, :], of_batch(x_v, b + 1)).then_inc(x_loaded, 16)
                for g in range(NG):
                    if ("k", g + 2) in jobs.place:
                        stack(jobs, b, g + 2)
                for t in range(NT):
                    wait_alone(sp, y1_done, b * NT + t + 1)
                    sp.dma_start(of_batch(y1_v, b)[:, t, :], z_tok[:, t, :]).then_inc(y1_stored, 16)
                if ahead:
                    wait_alone(sp, y1_stored, (b + 1) * (16 * NT))
                    sp.dma_start(z_tok[:, :, :], of_batch(x_v, b + 1)).then_inc(z_loaded, 16)

            with sp.Fori(0, B - 1) as b:
                batch(b, True)
            batch(B - 1, False)

            sp.wait_ge(y1_stored, 16 * B * NT)
            sp.dma_start(x_tok[:, :, :], y1_v[0]).then_inc(y_loaded, 16)
            sp.dma_start(z_tok[:, :, :], y1_v[0]).then_inc(r_loaded, 16)
            for r in range(FW_ROUNDS):
                if r >= 2:
                    sp.wait_ge(fw_shifted, (r - 1) * TPR)
                if r < NI // TPR:
                    src = gate_v[r]
                elif r < 2 * NI // TPR:
                    src = up_v[r - NI // TPR]
                else:
                    src = down_v[r - 2 * NI // TPR]
                sp.dma_start(w_int[:, r % 2, :, :], src).then_inc(fw_loaded[r % 2], 16)
            with nc.allow_non_contiguous_dma(reason="a scale per partition"):
                sp.dma_start(g_scale[:, :], gate_scale.rearrange("(c p) -> p c", p=P)).then_inc(scales_loaded, 16)
                sp.dma_start(u_scale[:, :], up_scale.rearrange("(c p) -> p c", p=P)).then_inc(scales_loaded, 16)
            sp.dma_start(d_scale[:, :], down_scale.partition_broadcast(P)).then_inc(scales_loaded, 16)

            def ffn_batch(b, ahead):
                if ahead:
                    wait_alone(sp, yT_full, (b + 1) * ND)
                    sp.dma_start(x_tok[:, :, :], of_batch(y1_v, b + 1)).then_inc(y_loaded, 16)
                for t in range(NT):
                    wait_alone(sp, out_done, b * NT + t + 1)
                    sp.dma_start(of_batch(out_v, b)[:, t, :], z_tok[:, t, :]).then_inc(out_stored, 16)
                if ahead:
                    wait_alone(sp, out_stored, (b + 1) * (16 * NT))
                    sp.dma_start(z_tok[:, :, :], of_batch(y1_v, b + 1)).then_inc(r_loaded, 16)

            with sp.Fori(0, B - 1) as b:
                ffn_batch(b, True)
            ffn_batch(B - 1, False)
            sp.wait_ge(out_stored, 16 * B * NT)

        @block.gpsimd
        def _(pool):
            nc.gpsimd.memset(ident[:, :], 0.0)
            nc.gpsimd.memset(causal[:, :], 0.0)
            nc.gpsimd.memset(half_power[:, :], -0.5).then_inc(pool_step, 1)
            pool.wait_ge(pool_step, 1)
            nc.gpsimd.affine_select(out=ident[:, :], in_=ident[:, :], compare_op=ALU.not_equal, fill=1.0, base=0,
                                    pattern=[[-1, P]], channel_multiplier=1)
            nc.gpsimd.affine_select(out=causal[:, S - P:S], in_=causal[:, S - P:S], compare_op=ALU.is_ge, fill=FLOOR,
                                    base=0, pattern=[[-1, P]], channel_multiplier=1).then_inc(consts_ready, 1)
            pool.wait_ge(bias_loaded, 16 * (HG + 2))

            def batch(b):
                for u in range(UNITS):
                    g, qb = divmod(u, NT)
                    wait_alone(pool, inv_done, b * UNITS + u + 1)
                    nc.gpsimd.tensor_copy(inv_wide[:, g % 2, qb, :, :],
                                          inv_sum[:, qb, :].unsqueeze(2).broadcast_to((P, HG, HD))).then_inc(inv_widened, 1)
                    if u == UNITS // 2:
                        pool.wait_ge(z_loaded, b * 16 + 16)
                        for t in range(NT):
                            last = nc.gpsimd.tensor_tensor(z_tok[:, t, :], z_tok[:, t, :], bias_o[:, :], ALU.add)
                        last.then_inc(res_ready, 1)
                pool.wait_ge(var_done, b + 1)
                nc.gpsimd.tensor_tensor(ln_rstd[:, :], ln_var[:, :], half_power[:, :], ALU.pow).then_inc(rstd_done, 1)

            with pool.Fori(0, B) as b:
                batch(b)
            with pool.Fori(0, B) as b:
                pool.wait_ge(var2_done, b + 1)
                nc.gpsimd.tensor_tensor(ln_rstd[:, :], ln_var[:, :], half_power[:, :], ALU.pow).then_inc(rstd2_done, 1)

        @block.scalar
        def _(act):
            act.wait_ge(consts_ready, 1)
            nc.scalar.activation(ln_rstd[:, :], half_power[:, :], ACT.Exp).then_inc(pT_evicted[0], 1)
            with act.Fori(0, NROUND // 2) as r:
                for s in range(TPR):
                    act.wait_ge(w_full, r * TPR + s + 1)
                    nc.scalar.activation(by_row(wT_hi, r * (TPR * P) + s * P),
                                         pj[s % 2][:, :].rearrange("p (c j d) -> p c j d", c=ND, j=HG),
                                         ACT.Copy).then_inc(w_hi_done, 1)
            with act.Fori(NROUND // 2, NROUND) as r:
                for s in range(TPR):
                    act.wait_ge(w_full, r * TPR + s + 1)
                    nc.scalar.activation(wT_hi[:, :, bass.ds(r * (TPR * P) + s * P, P)],
                                         pj[s % 2][:, :].rearrange("p (c e) -> p c e", c=ND),
                                         ACT.Copy).then_inc(w_hi_done, 1)
            act.wait_ge(bias_loaded, 16 * (HG + 2))

            def x_hi(jobs, c):
                act.wait_ge(pj_full[jobs.bank("x", c)], jobs.done("x", c))
                nc.scalar.activation(xT_hi[:, c, :], pj[jobs.bank("x", c)][:, :], ACT.Copy).then_inc(x_hi_done, 1)

            def qk_hi(jobs, b, kind, r):
                n = "qk".index(kind)
                act.wait_ge(pj_full[jobs.bank(kind, r)], jobs.done(kind, r))
                if r >= 1:
                    act.wait_ge(stacked, (b * NG + r) * STACK_DMAS)
                chunk = n * NG + r % NG
                nc.scalar.activation((q_hi, k_hi)[n][:, :], pj[jobs.bank(kind, r)][:, :], ACT.Identity,
                                     bias=bias_qk[:, chunk:chunk + 1]).then_inc(qk_hi_done, 1)

            def exponentials(b, u, j):
                act.wait_ge(neg_done, b * UNITS + u + 1)
                qb = u % NT
                nc.scalar.activation(probs[qb][:, j, :], probs[qb][:, j, :], ACT.Exp, bias=neg_max[:, qb, j:j + 1],
                                     scale=SCALE, accum_out=row_sum[:, qb, j:j + 1]).then_inc(exp_done, 1)

            def att_hi(b, g):
                act.wait_ge(att_done, b * NG + g + 3)
                nc.scalar.activation(attT_hi[:, g, :], attT[:, g % 2, :], ACT.Copy).then_inc(att_hi_done, 1)

            for c in range(ND):
                x_hi(front_jobs, c)
            for r in range(2):
                for kind in "qk":
                    qk_hi(front_jobs, 0, kind, r)
                    if r == 1 and kind == "q":
                        for j in range(HG):
                            exponentials(0, 0, j)

            def batch(b, ahead):
                jobs = jobs_of(b, ahead)
                for u in range(UNITS):
                    g, qb = divmod(u, NT)
                    for j in range(HG):
                        s = qb * HG + j
                        if j <= qb and block_of(u, j) % 2 == 0:
                            evict_block(act, 0, b, block_of(u, j),
                                        lambda o, i: nc.scalar.activation(o, i, ACT.Copy))
                        if j < HG // 2 and (ahead or u + 1 < UNITS):
                            exponentials(b, u + 1, 2 * j)
                            exponentials(b, u + 1, 2 * j + 1)
                        if g > 0 and s == 2:
                            att_hi(b, g - 1)
                        if ("q", g + 2) in jobs.place and s == 6:
                            qk_hi(jobs, b, "q", g + 2)
                        if ("k", g + 2) in jobs.place and s == 12:
                            qk_hi(jobs, b, "k", g + 2)
                        if ahead and g == NG - 3 and s >= 12:
                            x_hi(jobs, s - 12)
                att_hi(b, NG - 1)

            with act.Fori(0, B - 1) as b:
                batch(b, True)
            batch(B - 1, False)

            def y_hi(b, c):
                act.wait_ge(yT_full, b * ND + c + 1)
                nc.scalar.activation(xT_hi[:, c, :], y_bank[c][:, :], ACT.Copy).then_inc(yT_hi_done, 1)

            for n in range(0, NFW, 2):
                evict_ffn_weight(act, n, lambda o, i: nc.scalar.activation(o, i, ACT.Copy))
            act.wait_ge(scales_loaded, 48)
            for c in range(ND):
                y_hi(0, c)

            def ffn_batch(b, ahead):
                for i in range(NI):
                    act.wait_ge(gate_full, b * NI + i + 1)
                    nc.scalar.activation(silu[:, i % 2, :], gate_acc[i % 2][:, :], ACT.Silu,
                                         scale=g_scale[:, i:i + 1]).then_inc(silu_done, 1)
                    act.wait_ge(hid_done, b * NI + i + 1)
                    if i >= 2:
                        act.wait_ge(down_full, b * NI + i - 1)
                    nc.scalar.activation(hid_hi[:, i % 2, :], hid[:, i % 2, :], ACT.Copy).then_inc(hid_hi_done, 1)
                if ahead:
                    for c in range(ND):
                        y_hi(b + 1, c)

            with act.Fori(0, B - 1) as b:
                ffn_batch(b, True)
            ffn_batch(B - 1, False)

        @block.vector
        def _(dve):
            nc.vector.memset(ln_var[:, :], 1.0).then_inc(att_done, 2)
            nc.vector.memset(ln_stat[:, :, :], 0.0).then_inc(pT_evicted[1], 1)
            nc.vector.memset(ln_mv[:, :, :], 0.0).then_inc(d_done, 1)
            with dve.Fori(0, NROUND // 2) as r:
                for s in range(TPR):
                    first = r * (TPR * P) + s * P
                    dve.wait_ge(w_hi_done, r * TPR + s + 1)
                    nc.vector.tensor_tensor(by_row(wT_lo, first),
                                            pj[s % 2][:, :].rearrange("p (c j d) -> p c j d", c=ND, j=HG),
                                            by_row(wT_hi, first).bitcast(F32), ALU.subtract).then_inc(w_free, 1)
            with dve.Fori(NROUND // 2, NROUND) as r:
                for s in range(TPR):
                    col = bass.ds(r * (TPR * P) + s * P, P)
                    dve.wait_ge(w_hi_done, r * TPR + s + 1)
                    nc.vector.tensor_tensor(wT_lo[:, :, col], pj[s % 2][:, :].rearrange("p (c e) -> p c e", c=ND),
                                            wT_hi[:, :, col].bitcast(F32), ALU.subtract).then_inc(w_free, 1)
            dve.wait_ge(bias_loaded, 16 * (HG + 2))
            dve.wait_ge(consts_ready, 1)

            def x_lo(jobs, count, c):
                dve.wait_ge(x_hi_done, count + c + 1)
                nc.vector.tensor_tensor(xT_lo[:, c, :], pj[jobs.bank("x", c)][:, :], xT_hi[:, c, :].bitcast(F32),
                                        ALU.subtract).then_inc(pj_drained[jobs.bank("x", c)], 1)

            def qk_lo(jobs, b, kind, r):
                n = "qk".index(kind)
                chunk = n * NG + r % NG
                dve.wait_ge(qk_hi_done, (b * NG + r) * 2 + n + 1)
                nc.vector.scalar_tensor_tensor(
                    out=(q_lo, k_lo)[n][:, :], in0=pj[jobs.bank(kind, r)][:, :], scalar=bias_qk[:, chunk:chunk + 1],
                    in1=(q_hi, k_hi)[n][:, :].bitcast(F32), op0=ALU.add,
                    op1=ALU.subtract).then_inc(pj_drained[jobs.bank(kind, r)], 1)

            def values(jobs, t):
                dve.wait_ge(pj_full[jobs.bank("v", t)], jobs.done("v", t))
                nc.vector.tensor_tensor(v_tok[:, t, :], pj[jobs.bank("v", t)][:, :], bias_v[:, :],
                                        ALU.add).then_inc(pj_drained[jobs.bank("v", t)], 1)

            def tile_max(b, u, j):
                qb = u % NT
                w = P_WIDTH[qb]
                wait_alone(dve, score_full, (b * UNITS + u) * HG + j + 1)
                nc.vector.tensor_tensor_reduce(
                    out=probs[qb][:, j, :], in0=score[j % 2][:, 0:w], in1=causal[:, S - w:S], scale=1.0, scalar=FLOOR,
                    op0=ALU.add, op1=ALU.max, accum_out=row_max[:, qb, j:j + 1]).then_inc(max_done, 1)

            def negate_max(b, u):
                qb = u % NT
                dve.wait_ge(max_done, (b * UNITS + u + 1) * HG)
                nc.vector.tensor_scalar(neg_max[:, qb, :], row_max[:, qb, :], -SCALE, None, ALU.mult).then_inc(neg_done, 1)

            def inverse_sum(b, u):
                qb = u % NT
                dve.wait_ge(exp_done, (b * UNITS + u + 1) * HG)
                nc.vector.reciprocal(inv_sum[:, qb, :], row_sum[:, qb, :]).then_inc(inv_done, 1)

            def keep_inverse(jobs, g):
                dve.wait_ge(pj_full[jobs.bank("r", g)], jobs.done("r", g))
                nc.vector.tensor_copy(invT[:, :], pj[jobs.bank("r", g)][:, :]).then_inc(pj_drained[jobs.bank("r", g)], 1)

            def normalise(jobs, b, g):
                dve.wait_ge(pj_drained[jobs.bank("r", g)], jobs.done("r", g))
                dve.wait_ge(pv_full, b * NG + g + 1)
                nc.vector.tensor_tensor(attT[:, g % 2, :], pv_acc[g % 2][:, :], invT[:, :], ALU.mult).then_inc(att_done, 1)

            def att_lo(b, g):
                dve.wait_ge(att_hi_done, b * NG + g + 1)
                nc.vector.tensor_tensor(attT_lo[:, g, :], attT[:, g % 2, :], attT_hi[:, g, :].bitcast(F32),
                                        ALU.subtract).then_inc(att_ready, 1)

            def statistics(b, t, stat, mv):
                nc.vector.bn_stats(ln_stat[:, t, :], z_tok[:, t, :]).then_inc(stat, 1)
                wait_alone(dve, stat, b * NT + t + 1)
                nc.vector.bn_aggr(ln_mv[:, t, :], ln_stat[:, t, :]).then_inc(mv, 1)

            def layer_norm(b, mv, var, rstd, done):
                dve.wait_ge(mv, (b + 1) * NT)
                nc.vector.tensor_scalar(ln_var[:, :], ln_mv[:, :, 1], EPS, None, ALU.add).then_inc(var, 1)
                dve.wait_ge(rstd, b + 1)
                for t in range(NT):
                    nc.vector.tensor_scalar(z_tok[:, t, :], z_tok[:, t, :], ln_mv[:, t, 0:1], ln_rstd[:, t:t + 1],
                                            ALU.subtract, ALU.mult).then_inc(done, 1)

            for c in range(ND):
                x_lo(front_jobs, 0, c)
            for kind in "qk":
                qk_lo(front_jobs, 0, kind, 0)
            for t in range(NT):
                values(front_jobs, t)
            for u in range(AHEAD):
                for j in range(HG):
                    tile_max(0, u, j)
                negate_max(0, u)
                qk_lo(front_jobs, 0, "qk"[u], 1)
            inverse_sum(0, 0)

            def batch(b, ahead):
                jobs = jobs_of(b, ahead)
                for u in range(UNITS):
                    g, qb = divmod(u, NT)
                    for j in range(HG):
                        s = qb * HG + j
                        if ahead or u + AHEAD < UNITS:
                            tile_max(b, u + AHEAD, j)
                        if j <= qb and block_of(u, j) % 2 == 1:
                            evict_block(dve, 1, b, block_of(u, j), nc.vector.tensor_copy)
                        if j == 2 and (ahead or u + 1 < UNITS):
                            inverse_sum(b, u + 1)
                        if g > 0 and s == 1:
                            normalise(jobs, b, g - 1)
                        if g > 0 and s == 3:
                            att_lo(b, g - 1)
                        if s == 13:
                            keep_inverse(jobs, g)
                        if ("q", g + 2) in jobs.place and s == 6:
                            qk_lo(jobs, b, "q", g + 2)
                        if ("k", g + 2) in jobs.place and s == 12:
                            qk_lo(jobs, b, "k", g + 2)
                        if ahead and g == NG - 3 and s >= 12:
                            x_lo(jobs, (b + 1) * ND, s - 12)
                    if ahead or u + AHEAD < UNITS:
                        negate_max(b, u + AHEAD)
                normalise(jobs, b, NG - 1)
                att_lo(b, NG - 1)
                if ahead:
                    for t in range(NT):
                        values(jobs, t)
                dve.wait_ge(res_ready, b + 1)
                for t in range(NT):
                    dve.wait_ge(pj_full[jobs.bank("o", t)], jobs.done("o", t))
                    nc.vector.tensor_tensor(z_tok[:, t, :], pj[jobs.bank("o", t)][:, :], z_tok[:, t, :],
                                            ALU.add).then_inc(pj_drained[jobs.bank("o", t)], 1)
                    dve.wait_ge(pj_drained[jobs.bank("o", t)], jobs.done("o", t))
                    statistics(b, t, stat_done, mv_done)
                layer_norm(b, mv_done, var_done, rstd_done, y1_done)

            with dve.Fori(0, B - 1) as b:
                batch(b, True)
            batch(B - 1, False)

            for n in range(NFW):
                shift_ffn_weight(dve, n)
                if n >= 2 and (n - 2) % 2 == 1:
                    evict_ffn_weight(dve, n - 2, nc.vector.tensor_copy)
            evict_ffn_weight(dve, NFW - 1, nc.vector.tensor_copy)
            dve.wait_ge(scales_loaded, 48)

            def y_lo(b, c):
                dve.wait_ge(yT_hi_done, b * ND + c + 1)
                nc.vector.tensor_tensor(xT_lo[:, c, :], y_bank[c][:, :], xT_hi[:, c, :].bitcast(F32),
                                        ALU.subtract).then_inc(yT_done, 1)

            for c in range(ND):
                y_lo(0, c)

            def ffn_batch(b, ahead):
                for i in range(NI):
                    dve.wait_ge(up_full, b * NI + i + 1)
                    dve.wait_ge(silu_done, b * NI + i + 1)
                    nc.vector.scalar_tensor_tensor(out=hid[:, i % 2, :], in0=up_acc[i % 2][:, :],
                                                   scalar=u_scale[:, i:i + 1], in1=silu[:, i % 2, :], op0=ALU.mult,
                                                   op1=ALU.mult).then_inc(hid_done, 1)
                    dve.wait_ge(hid_hi_done, b * NI + i + 1)
                    nc.vector.tensor_tensor(hid_lo[:, i % 2, :], hid[:, i % 2, :], hid_hi[:, i % 2, :].bitcast(F32),
                                            ALU.subtract).then_inc(hid_ready, 1)
                if ahead:
                    for c in range(ND):
                        y_lo(b + 1, c)
                dve.wait_ge(r_loaded, b * 16 + 16)
                dve.wait_ge(down_full, (b + 1) * NI)
                for t in range(NT):
                    nc.vector.tensor_tensor(d_scaled[:, t % 2, :], down_acc[t][:, :], d_scale[:, :],
                                            ALU.mult).then_inc(d_done, 1)
                    dve.wait_ge(d_done, b * NT + t + 2)
                    nc.vector.tensor_tensor(z_tok[:, t, :], d_scaled[:, t % 2, :], z_tok[:, t, :],
                                            ALU.add).then_inc(z2_done, 1)
                    dve.wait_ge(z2_done, b * NT + t + 1)
                    statistics(b, t, stat2_done, mv2_done)
                layer_norm(b, mv2_done, var2_done, rstd2_done, out_done)

            with dve.Fori(0, B - 1) as b:
                ffn_batch(b, True)
            ffn_batch(B - 1, False)

        def split_product(acc, a_hi, a_lo, b_hi, b_lo, first, last):
            nc.tensor.matmul(acc, a_hi, b_hi, start=first, stop=False)
            nc.tensor.matmul(acc, a_hi, b_lo, start=False, stop=False)
            return nc.tensor.matmul(acc, a_lo, b_hi, start=False, stop=last)

        @block.tensor
        def _(pe):
            pe.wait_ge(consts_ready, 1)
            for r in range(NROUND):
                pe.wait_ge(w_loaded[r], 16)
                for s in range(TPR):
                    n = r * TPR + s
                    if n >= 2:
                        pe.wait_ge(w_free, n - 1)
                    for c in range(ND):
                        last = nc.tensor.transpose(pj[n % 2][:, c * P:(c + 1) * P], w_stage[r % 3][:, s, c * P:(c + 1) * P],
                                                   ident[:, :])
                    last.then_inc(w_full, 1)
            pe.wait_ge(w_free, NROUND * TPR)

            def bank_for(jobs, *job):
                if jobs.before_it(*job) is not None:
                    pe.wait_ge(pj_drained[jobs.bank(*job)], jobs.before_it(*job))
                return pj[jobs.bank(*job)]

            def transpose_x(jobs, b, c):
                if c == 0:
                    pe.wait_ge(x_loaded, b * 16 + 16)
                acc = bank_for(jobs, "x", c)
                for t in range(NT):
                    last = nc.tensor.transpose(acc[:, t * P:(t + 1) * P], x_tok[:, t, c * P:(c + 1) * P], ident[:, :])
                last.then_inc(pj_full[jobs.bank("x", c)], 1)

            def project(jobs, x_jobs, r):
                for n, kind in enumerate("qk"):
                    acc = bank_for(jobs, kind, r)
                    e = slice(n * D + r % NG * P, n * D + (r % NG + 1) * P)
                    for c in range(ND):
                        if x_jobs is not None and n == 0:
                            pe.wait_ge(pj_drained[x_jobs.bank("x", c)], x_jobs.done("x", c))
                        first, final = c == 0, c == ND - 1
                        nc.tensor.matmul(acc[:, :], wT_hi[:, c, e], xT_hi[:, c, :], start=first, stop=False)
                        yield
                        nc.tensor.matmul(acc[:, :], wT_hi[:, c, e], xT_lo[:, c, :], start=False, stop=False)
                        yield
                        last = nc.tensor.matmul(acc[:, :], wT_lo[:, c, e], xT_hi[:, c, :], start=False, stop=final)
                        if final:
                            last.then_inc(pj_full[jobs.bank(kind, r)], 1)
                        yield

            def project_values(jobs, t):
                acc = bank_for(jobs, "v", t)
                tok = slice(t * P, (t + 1) * P)
                for c in range(ND):
                    last = split_product(acc[:, :], xT_hi[:, c, tok], xT_lo[:, c, tok], wT_hi[:, c, 2 * D:3 * D],
                                         wT_lo[:, c, 2 * D:3 * D], c == 0, c == ND - 1)
                last.then_inc(pj_full[jobs.bank("v", t)], 1)

            def scores(b, u, j):
                r, qb = divmod(u, NT)
                n = (b * UNITS + u) * HG + j
                w = P_WIDTH[qb]
                if qb == 0 and j == 0:
                    pe.wait_ge(stacked, (b * NG + r + 1) * STACK_DMAS)
                if u > 0 or j >= 2:
                    pe.wait_ge(max_done, n - 1)
                nc.tensor.matmul(score[j % 2][:, 0:w], q_stack[r % 2][:, j, qb * P:(qb + 1) * P],
                                 k_stack[r % 2][:, j, 0:w], start=True, stop=True).then_inc(score_full, 1)

            def transpose_block(b, u, kb):
                n = block_of(u, kb)
                qb = u % NT
                pe.wait_ge(pT_evicted[n % 2], b * (NG * BLOCKS // 2) + n // 2 + 1)
                for j in range(HG):
                    if kb == 0:
                        pe.wait_ge(exp_done, (b * UNITS + u) * HG + j + 1)
                    last = nc.tensor.transpose(pT[n % 2][:, j * P:(j + 1) * P], probs[qb][:, j, kb * P:(kb + 1) * P],
                                               ident[:, :])
                last.then_inc(pT_full, 1)

            def weighted_values(b, u, kb):
                n = block_of(u, kb)
                g, qb = divmod(u, NT)
                if qb == 0:
                    pe.wait_ge(att_done, b * NG + g + 1)
                pe.wait_ge(pT_evicted[n % 2], b * (NG * BLOCKS // 2) + n // 2 + 2)
                for j in range(HG):
                    h = g * HG + j
                    last = nc.tensor.matmul(pv_acc[g % 2][j * HD:(j + 1) * HD, qb * P:(qb + 1) * P],
                                            v_tok[:, kb, h * HD:(h + 1) * HD], probsT[:, n % 4, j, :],
                                            start=kb == 0, stop=kb == qb)
                if qb == NT - 1 and kb == qb:
                    last.then_inc(pv_full, 1)

            def transpose_inverse(jobs, b, g):
                acc = bank_for(jobs, "r", g)
                pe.wait_ge(inv_widened, b * UNITS + (g + 1) * NT)
                for qb in range(NT):
                    last = nc.tensor.transpose(acc[:, qb * P:(qb + 1) * P],
                                               inv_wide[:, g % 2, qb, :, :].rearrange("p j d -> p (j d)"), ident[:, :])
                last.then_inc(pj_full[jobs.bank("r", g)], 1)

            for c in range(ND):
                transpose_x(front_jobs, 0, c)
            for _ in project(front_jobs, front_jobs, 0):
                pass
            for t in range(NT):
                project_values(front_jobs, t)
            work = project(front_jobs, None, 1)
            for u in range(AHEAD):
                for j in range(HG):
                    scores(0, u, j)
                    for _ in range(3):
                        next(work)
            next(work, None)

            def batch(b, ahead):
                jobs = jobs_of(b, ahead)
                waiting = None
                for u in range(UNITS):
                    g, qb = divmod(u, NT)
                    if qb == 0 and ("q", g + 2) in jobs.place:
                        work = project(jobs, jobs if g + 2 == NG else None, g + 2)
                    for j in range(HG):
                        s = qb * HG + j
                        if ahead or u + AHEAD < UNITS:
                            scores(b, u + AHEAD, j)
                        if j <= qb:
                            transpose_block(b, u, j)
                        if waiting:
                            weighted_values(b, *waiting)
                        waiting = (u, j) if j <= qb else None
                        if ("q", g + 2) in jobs.place and s < 12:
                            next(work)
                            next(work)
                            if s == 11:
                                next(work, None)
                        if s == 12:
                            transpose_inverse(jobs, b, g)
                        if ahead and g == NG - 3 and s >= 12:
                            transpose_x(jobs, b + 1, s - 12)
                weighted_values(b, *waiting)
                if ahead:
                    for t in range(NT):
                        project_values(jobs, t)
                pe.wait_ge(att_ready, (b + 1) * NG)
                for t in range(NT):
                    acc = bank_for(jobs, "o", t)
                    tok = slice(t * P, (t + 1) * P)
                    for c in range(NG):
                        last = split_product(acc[:, :], attT_hi[:, c, tok], attT_lo[:, c, tok], wT_hi[:, c, NE:NE + D],
                                             wT_lo[:, c, NE:NE + D], c == 0, c == NG - 1)
                    last.then_inc(pj_full[jobs.bank("o", t)], 1)

            with pe.Fori(0, B - 1) as b:
                batch(b, True)
            batch(B - 1, False)

            last_jobs = jobs_of(B - 1, False)
            for n in range(NFW):
                pe.wait_ge(fw_shifted, n + 1)
                if n >= 2:
                    pe.wait_ge(fw_free[n % 2], n // 2)
                else:
                    t = NT - 2 + n
                    pe.wait_ge(pj_drained[last_jobs.bank("o", t)], last_jobs.done("o", t))
                for c in range(TPR):
                    last = nc.tensor.transpose(pj[n % 2][:, c * P:(c + 1) * P], w_shift[:, n % 2, c * P:(c + 1) * P],
                                               ident[:, :])
                last.then_inc(fw_full, 1)
            for i in range(2):
                pe.wait_ge(fw_free[i], NFW // 2)

            def transpose_y(b, c):
                if c == 0:
                    pe.wait_ge(y_loaded, b * 16 + 16)
                for t in range(NT):
                    last = nc.tensor.transpose(y_bank[c][:, t * P:(t + 1) * P], x_tok[:, t, c * P:(c + 1) * P], ident[:, :])
                last.then_inc(yT_full, 1)

            for c in range(ND):
                transpose_y(0, c)

            def ffn_batch(b, ahead):
                def gate_up(i):
                    cols = slice(i * P, (i + 1) * P)
                    if i >= 2:
                        pe.wait_ge(hid_done, b * NI + i - 1)
                    for w, acc, full in ((gateT, gate_acc, gate_full), (upT, up_acc, up_full)):
                        for c in range(ND):
                            if i == 0 and w is gateT:
                                pe.wait_ge(yT_done, b * ND + (c + 1 if c else 1))
                            nc.tensor.matmul(acc[i % 2][:, :], w[:, c, cols], xT_hi[:, c, :], start=c == 0, stop=False)
                            last = nc.tensor.matmul(acc[i % 2][:, :], w[:, c, cols], xT_lo[:, c, :], start=False,
                                                    stop=c == ND - 1)
                        last.then_inc(full, 1)

                def down(i):
                    pe.wait_ge(hid_ready, b * NI + i + 1)
                    if i == 0:
                        pe.wait_ge(d_done, b * NT + 1)
                    for t in range(NT):
                        tok = slice(t * P, (t + 1) * P)
                        nc.tensor.matmul(down_acc[t][:, :], hid_hi[:, i % 2, tok], downT[:, i, :], start=i == 0, stop=False)
                        last = nc.tensor.matmul(down_acc[t][:, :], hid_lo[:, i % 2, tok], downT[:, i, :], start=False,
                                                stop=i == NI - 1)
                    last.then_inc(down_full, 1)

                gate_up(0)
                for i in range(1, NI):
                    gate_up(i)
                    down(i - 1)
                if ahead:
                    pe.wait_ge(hid_done, b * NI + NI - 1)
                    transpose_y(b + 1, 0)
                    transpose_y(b + 1, 1)
                down(NI - 1)
                if ahead:
                    pe.wait_ge(hid_done, b * NI + NI)
                    transpose_y(b + 1, 2)
                    transpose_y(b + 1, 3)

            with pe.Fori(0, B - 1) as b:
                ffn_batch(b, True)
            ffn_batch(B - 1, False)


_INS = ['L0_attn_x', 'L0_attn_w_qkv', 'L0_attn_b_qkv', 'L0_attn_w_out', 'L0_attn_b_out', 'L0_ffn_gate_w',
        'L0_ffn_gate_scale', 'L0_ffn_up_w', 'L0_ffn_up_scale', 'L0_ffn_down_w', 'L0_ffn_down_scale']


def kernel(**inputs):
    import numpy as _np
    import concourse.bacc as _bacc
    from concourse import mybir as _mybir
    from concourse.bass_utils import run_bass_kernel_spmd as _run

    nc = _bacc.Bacc("TRN2", target_bir_lowering=False, num_devices=1)
    arrays, args = {}, []
    for name in _INS:
        a = _np.ascontiguousarray(inputs[name])
        arrays[f"in_{name}_dram"] = a
        args.append(nc.dram_tensor(f"in_{name}_dram", a.shape, _mybir.dt.from_np(a.dtype), kind="ExternalInput").ap())
    shape = inputs['L0_attn_x'].shape
    args.append(nc.dram_tensor("out_0_dram", shape, _mybir.dt.float32, kind="ExternalOutput").ap())
    postln_block_kernel(nc, *args)
    r = _run(nc, [arrays], core_ids=[0])
    return r.results[0]["out_0_dram"]
```

```python
import concourse.bass as bass
from concourse import mybir
from contextlib import ExitStack
from itertools import chain


def postln_block_kernel(nc: bass.Bass, x, w_qkv, b_qkv, w_out, b_out, gate_w, gate_scale, up_w, up_scale,
                        down_w, down_scale, out):
    F32, F32R, I32, U32 = mybir.dt.float32, mybir.dt.float32r, mybir.dt.int32, mybir.dt.uint32
    ALU, ACT = mybir.AluOpType, mybir.ActivationFunctionType

    P = 128
    B, S, D = x.shape
    HD = 32
    H = D // HD
    I = gate_w.shape[0]
    ND = D // P
    NT = S // P
    NI = I // P
    HG = P // HD
    NG = H // HG
    NE = 3 * D
    UNITS = NG * NT
    BLOCKS = NT * (NT + 1) // 2
    NORM_AT = 5
    STEPS = NT * HG
    PLACE_STEPS = [0, 2, 5, 7]
    X_STEPS = [8, 10, 12, 14]
    AHEAD = 2
    SCALE = float(HD) ** -0.5
    EPS = 1e-5
    ZERO_POINT = 128.0
    EXACT = 4096
    FLOOR = -3.0e38
    TPR = 4
    NROUND = (NE + D) // (P * TPR)
    STACK = 3 * HD
    STACK_DMAS = 6 * 16

    FRONT = ([("x", c) for c in range(ND)] + [("q", 0), ("k", 0)] + [("v", t) for t in range(NT)] +
             [("q", 1), ("k", 1)])

    def filling(first, ahead, g):
        jobs = [("q", g + 2), ("k", g + 2)] if ahead or g + 2 < NG else []
        if g == 0 and not first:
            return jobs + [("o", t) for t in range(NT)], [6] * 8 + [3] * 8
        if g == NG - 2 and ahead:
            return jobs + [("v", 0), ("v", 1)], [0, 0] + [3, 4] * 6 + [3, 3]
        if g == NG - 1 and ahead:
            return jobs + [("v", 2), ("v", 3)], [3] * 4 + [4] * 4 + [3] * 4 + [2] * 4
        if g == NG - 3:
            return jobs, [3] * 8 + [0] * 8
        return jobs, [2] * 12 + [0] * 4 if jobs else [0] * STEPS

    def filled(first, ahead):
        over = {}
        for g in range(NG):
            jobs, counts = filling(first, ahead, g)
            for n, job in enumerate(jobs):
                step = next(s for s in range(STEPS) if sum(counts[:s + 1]) >= 3 * ND * (n + 1))
                over.setdefault(g * STEPS + step + 1, []).append(job)
        return over

    def batch_jobs(first, ahead):
        jobs = []
        for g in range(NG):
            jobs += filling(first, ahead, g)[0]
            if g == NG - 3:
                jobs += [("x", c) for c in range(ND)]
            jobs += [("r", g)]
        return jobs if ahead else jobs + [("f", t) for t in range(NT)]

    IN_FIRST, PER_BATCH = len(batch_jobs(True, True)), len(batch_jobs(False, True))
    assert IN_FIRST % 2 == 0 and PER_BATCH % 2 == 0

    class Jobs:

        def __init__(self, batches, jobs, before):
            self.batches = batches
            self.place = {job: before + n for n, job in enumerate(jobs)}

        def bank(self, *job):
            return self.place[job] % 2

        def done(self, *job):
            return self.batches * (PER_BATCH // 2) + self.place[job] // 2 + 1

        def before_it(self, *job):
            return None if self.place[job] < 2 else self.done(*job) - 1

    front_jobs = Jobs(0, FRONT, 0)

    def jobs_of(b, first, ahead):
        if first:
            return Jobs(0, batch_jobs(True, ahead), len(FRONT))
        return Jobs(b - 1, batch_jobs(False, ahead), len(FRONT) + IN_FIRST)

    def jobs_before(b):
        return Jobs(b - 1, batch_jobs(False, True), len(FRONT) + IN_FIRST - PER_BATCH)

    y1_dram = nc.dram_tensor("y1_scratch", (B * S, D), F32, kind="Internal").ap()
    x_v = x.rearrange("b (t p) d -> b p t d", p=P)
    y1_v = y1_dram.rearrange("(b t p) d -> b p t d", p=P, t=NT)
    out_v = out.rearrange("b (t p) d -> b p t d", p=P)
    assert NI // TPR == B
    scan_v = [w.rearrange("(r t p) c -> r p t c", p=P, t=TPR) for w in (gate_w, up_w)] + [
        down_w.rearrange("(t p) (r c) -> r p t c", p=P, c=TPR * P)]
    gate_v = gate_w.rearrange("(i p) d -> i p d", p=P)
    up_v = up_w.rearrange("(i p) d -> i p d", p=P)
    down_v = down_w.rearrange("(t p) (r c) -> r t p c", p=P, c=TPR * P)

    FIRST_PIECES = [("g", 0), ("u", 0)] + [("d", 0, t) for t in range(ND)]

    def pieces_at(i):
        r, t = i // TPR + 1, i % TPR
        return ([("g", i + 1), ("u", i + 1)] if i + 1 < NI else []) + [("d", r, t) if r < NI // TPR else ("y", t)]

    PIECES = FIRST_PIECES + [p for i in range(NI) for p in pieces_at(i)]
    WEIGHTS = [p for p in PIECES if p[0] != "y"]
    INTS = 10
    HIDS = NT
    SHIFTS = 4
    TURNS = list(range(9)) + [("y", 0)] + list(range(9, 12)) + [("y", 2)] + list(range(12, NI))

    LAST = B - 1
    PER_SCAN = 2
    SCANS = len(scan_v) * PER_SCAN
    SCAN_STEPS = [2 * STEPS + 9, 2 * STEPS + 11, 3 * STEPS + 5, 3 * STEPS + 7]
    LATE_SCAN_STEPS = [2, 4]

    def of_batch(view, b):
        return view[bass.ds(b, 1)].rearrange("o p t d -> (o p) t d")

    ctx = ExitStack()
    with ctx:
        def sb(name, shape, dt=F32, where=ctx):
            return where.enter_context(nc.sbuf_tensor(name, shape, dt))

        def sem(name):
            return ctx.enter_context(nc.semaphore(name))

        def sem_pair(name):
            return [sem(f"{name}{i}") for i in range(2)]

        ident = sb("ident", [P, P])
        x_tok = sb("x_tok", [P, NT, D])
        xT_hi = sb("xT_hi", [P, ND, S], F32R)
        xT_lo = sb("xT_lo", [P, ND, S], F32R)
        z_tok = sb("z_tok", [P, NT, D])
        scan_rows = sb("scan_rows", [P, 1])
        scan_top = sb("scan_top", [1, 1])
        wide_flag = sb("wide_flag", [1, 1], I32)
        ln_stat = sb("ln_stat", [P, NT, 6])
        ln_mv = sb("ln_mv", [P, NT, 2])
        ln_var = sb("ln_var", [P, NT])
        ln_rstd = sb("ln_rstd", [P, NT])
        half_power = sb("half_power", [P, NT])

        att = ExitStack()
        q_stack = [sb(f"q_stack{i}", [STACK, HG, S], F32R, att) for i in range(2)]
        k_stack = [sb(f"k_stack{i}", [STACK, HG, S], F32R, att) for i in range(2)]
        wT_hi = sb("wT_hi", [P, ND, NE + D], F32R, att)
        wT_lo = sb("wT_lo", [P, ND, NE + D], F32R, att)
        q_hi = sb("q_hi", [P, S], F32R, att)
        q_lo = sb("q_lo", [P, S], F32R, att)
        k_hi = sb("k_hi", [P, S], F32R, att)
        k_lo = sb("k_lo", [P, S], F32R, att)
        v_tok = sb("v_tok", [P, NT, D], F32, att)
        v_next = sb("v_next", [P, NT, D], F32, att)
        attT_hi = sb("attT_hi", [P, NG, S], F32R, att)
        attT_lo = sb("attT_lo", [P, NG, S], F32R, att)
        causal = sb("causal", [P, S], F32, att)
        row_max = sb("row_max", [P, NT, HG], F32, att)
        neg_max = sb("neg_max", [P, NT, HG], F32, att)
        row_sum = sb("row_sum", [P, NT, HG], F32, att)
        inv_sum = sb("inv_sum", [P, 2, NT, HG], F32, att)
        inv_wide = sb("inv_wide", [P, NT + 1, HG, HD], F32, att)
        invT = sb("invT", [P, S], F32, att)
        attT = sb("attT", [P, S], F32, att)
        scan_sums = sb("scan_sums", [P, B * SCANS], F32, att)
        scan_excess = sb("scan_excess", [P, TPR * D // PER_SCAN], mybir.dt.bfloat16, att)
        minus_exact = sb("minus_exact", [P, 1], F32, att)
        bias_qk = sb("bias_qk", [P, 2 * NG], F32, att)
        bias_v = sb("bias_v", [P, D], F32, att)
        bias_o = sb("bias_o", [P, D], F32, att)
        P_WIDTH = [(qb + 1) * P for qb in range(NT)]
        P_FIRST = [HG * sum(P_WIDTH[:qb]) for qb in range(NT)]
        probs_sb = sb("probs_sb", [P, HG * sum(P_WIDTH)], F32, att)
        probs = [probs_sb[:, P_FIRST[qb]:P_FIRST[qb] + HG * P_WIDTH[qb]].rearrange("p (j k) -> p j k", j=HG)
                 for qb in range(NT)]
        probsT = sb("probsT", [P, 2, HG, P], F32, att)
        w_stage = [t.rearrange("p (s d) -> p s d", s=TPR) for t in
                   (probs_sb[:, 0:TPR * D], probs_sb[:, TPR * D:2 * TPR * D],
                    v_next.rearrange("p t d -> p (t d)"))] + [z_tok[:, :, :]]
        att.close()

        ffn = ExitStack()
        w_int = sb("w_int", [P, INTS, D], I32, ffn)
        w_shift = sb("w_shift", [P, SHIFTS, D], F32, ffn)
        d_scale = sb("d_scale", [P, D], F32, ffn)
        g_scale = sb("g_scale", [P, NI], F32, ffn)
        u_scale = sb("u_scale", [P, NI], F32, ffn)
        d_scaled = sb("d_scaled", [P, NT, D], F32, ffn)
        gateT = sb("gateT", [P, ND, I], F32R, ffn)
        upT = sb("upT", [P, ND, I], F32R, ffn)
        downT = sb("downT", [P, NI, D], F32R, ffn)
        yT_next = sb("yT_next", [P, ND, S], F32, ffn)
        silu = sb("silu", [P, 2, S], F32, ffn)
        hid = sb("hid", [P, 2, S], F32, ffn)
        hid_hi = sb("hid_hi", [P, HIDS, S], F32R, ffn)
        hid_lo = sb("hid_lo", [P, HIDS, S], F32R, ffn)
        ffn.close()

        raw = ExitStack()
        sb("ahead_of_weights", [P, (INTS + SHIFTS + 1 + NT) * D + 2 * NI], F32, raw)
        gateT_wide = sb("gateT_wide", [P, ND, I], F32, raw)
        upT_wide = sb("upT_wide", [P, ND, I], F32, raw)
        downT_wide = sb("downT_wide", [P, NI, D], F32, raw)
        raw.close()
        exact_weights, wide_weights = (gateT, upT, downT), (gateT_wide, upT_wide, downT_wide)

        bank = [ctx.enter_context(nc.psum_tensor(f"bank{i}", [P, 512], F32)) for i in range(8)]
        pj, score, pT, pv_acc = bank[0:2], bank[2:4], bank[4:6], bank[6:8]
        w_bank = bank[2:6]
        gate_acc, up_acc, down_acc = bank[0:4:2], bank[1:4:2], bank[4:8]
        piece_bank = [gate_acc[1], up_acc[1]]

        consts_ready = sem("consts_ready")
        pool_step = sem("pool_step")
        bias_loaded = sem("bias_loaded")
        w_first = [sem(f"w_first{s}") for s in range(TPR)]
        w_loaded = [sem(f"w_loaded{r}") for r in range(NROUND)]
        w_full = sem("w_full")
        w_hi_done = sem("w_hi_done")
        w_free = sem("w_free")
        x_loaded = sem("x_loaded")
        z_loaded = sem("z_loaded")
        res_ready = sem("res_ready")
        pj_full = sem_pair("pj_full")
        pj_drained = sem_pair("pj_drained")
        x_hi_done = sem("x_hi_done")
        qk_hi_done = sem("qk_hi_done")
        stacked = sem("stacked")
        score_full = sem("score_full")
        max_done = sem("max_done")
        neg_done = sem("neg_done")
        exp_done = sem("exp_done")
        inv_done = sem("inv_done")
        inv_widened = sem("inv_widened")
        pT_full = sem("pT_full")
        pT_evicted = [sem("pT_evicted_act"), sem("pT_evicted_dve")]
        pv_full = sem("pv_full")
        v_placed = sem("v_placed")
        inv_kept = sem("inv_kept")
        att_hi_done = sem("att_hi_done")
        att_ready = sem("att_ready")
        stat_done = sem("stat_done")
        mv_done = sem("mv_done")
        var_done = sem("var_done")
        rstd_done = sem("rstd_done")
        y1_done = sem("y1_done")
        y1_stored = sem("y1_stored")
        scan_loaded = sem("scan_loaded")
        scanned = sem("scanned")
        scan_rows_done = sem("scan_rows_done")
        scan_top_done = sem("scan_top_done")
        scan_done = sem("scan_done")
        scales_loaded = sem("scales_loaded")
        fw_loaded = [sem(f"fw_loaded{i}") for i in range(INTS)]
        fw_shifted = sem("fw_shifted")
        piece_full = sem("piece_full")
        fw_placed = sem("fw_placed")
        yT_kept = sem("yT_kept")
        y_loaded = sem("y_loaded")
        r_loaded = sem("r_loaded")
        yT_full = sem("yT_full")
        yT_hi_done = sem("yT_hi_done")
        yT_done = sem("yT_done")
        gate_full = sem("gate_full")
        up_full = sem("up_full")
        silu_done = sem("silu_done")
        hid_done = sem("hid_done")
        hid_hi_done = sem("hid_hi_done")
        hid_ready = sem("hid_ready")
        down_full = sem("down_full")
        d_done = sem("d_done")
        z2_done = sem("z2_done")
        stat2_done = sem("stat2_done")
        mv2_done = sem("mv2_done")
        var2_done = sem("var2_done")
        rstd2_done = sem("rstd2_done")
        out_done = sem("out_done")
        out_stored = sem("out_stored")

        def wait_alone(eng, sem, value):
            value = eng.to_reg(value) if not isinstance(value, int) else value
            eng.wait_ge(consts_ready, 1)
            eng.wait_ge(sem, value)

        def turns_of(ahead):
            return TURNS if ahead else list(range(NI))

        def piece_place(piece, weights):
            gateT, upT, downT = weights
            kind, n = piece[:2]
            if kind == "g":
                return gateT[:, :, n * P:(n + 1) * P]
            if kind == "u":
                return upT[:, :, n * P:(n + 1) * P]
            if kind == "d":
                return downT[:, TPR * n:TPR * (n + 1), piece[2] * P:(piece[2] + 1) * P]
            return yT_next[:, n, :].rearrange("p (t q) -> p t q", t=NT)

        def piece_evicted(piece):
            if piece[0] == "y":
                return yT_kept, piece[1] + 1
            return fw_placed, WEIGHTS.index(piece) + 1

        def evict_block(eng, parity, b, n, copy):
            eng.wait_ge(pT_full, b * (NG * BLOCKS) + n + 1)
            copy(probsT[:, n % 2, :, :], pT[parity][:, :].rearrange("p (j q) -> p j q", j=HG)).then_inc(
                pT_evicted[parity], 1)

        def wide_place(g, qb):
            return qb if qb else NT * (g % 2)

        def block_of(u, kb):
            g, qb = divmod(u, NT)
            return g * BLOCKS + qb * (qb + 1) // 2 + kb

        def by_row(wT, first):
            return wT[:, :, bass.ds(first, P)].rearrange("p c (d j) -> p c j d", j=HG)

        block = ctx.enter_context(nc.Block())

        @block.sync
        def _(sp):
            def load_w(r):
                src = w_qkv[r * TPR * P:(r + 1) * TPR * P, :] if r < NE // (TPR * P) else w_out
                sp.dma_start(w_stage[r], src.rearrange("(s p) d -> p s d", p=P)).then_inc(w_loaded[r], 16)

            for s in range(TPR):
                sp.dma_start(w_stage[0][:, s, :], w_qkv[s * P:(s + 1) * P, :]).then_inc(w_first[s], 16)
            load_w(1)
            sp.dma_start(x_tok[:, :, :], x_v[0]).then_inc(x_loaded, 16)
            with nc.allow_non_contiguous_dma(reason="a bias per partition"):
                for j in range(HG):
                    sp.dma_start(bias_qk[j:P:HG, :],
                                 b_qkv[0:2 * D].rearrange("(c j d) -> j d c", j=HG, d=HD)[j]).then_inc(bias_loaded, 16)
            sp.dma_start(bias_v[:, :], b_qkv[2 * D:3 * D].partition_broadcast(P)).then_inc(bias_loaded, 16)
            sp.dma_start(bias_o[:, :], b_out.partition_broadcast(P)).then_inc(bias_loaded, 16)
            for r in range(2, NROUND):
                load_w(r)
            sp.wait_ge(w_full, NROUND * TPR)
            sp.dma_start(z_tok[:, :, :], x_v[0]).then_inc(z_loaded, 16)

            def stack(jobs, b, r):
                wait_alone(sp, pj_drained[jobs.bank("k", r)], jobs.done("k", r))
                if r >= 2:
                    wait_alone(sp, score_full, b * (UNITS * HG) + (r - 1) * (NT * HG))
                for n, (qs, ks) in enumerate(((q_hi, k_hi), (q_hi, k_lo), (q_lo, k_hi))):
                    to = slice(HD * n, HD * (n + 1))
                    sp.dma_start(q_stack[r % 2][to, :, :].bitcast(F32), qs[:, :].bitcast(F32)).then_inc(stacked, 16)
                    sp.dma_start(k_stack[r % 2][to, :, :].bitcast(F32), ks[:, :].bitcast(F32)).then_inc(stacked, 16)

            stack(front_jobs, 0, 0)
            stack(front_jobs, 0, 1)

            def store_y1(b):
                for t in range(NT):
                    wait_alone(sp, y1_done, b * NT + t + 1)
                    sp.dma_start(of_batch(y1_v, b)[:, t, :], z_tok[:, t, :]).then_inc(y1_stored, 16)

            def load_scan(b, k):
                if k > 0:
                    wait_alone(sp, scanned, b * SCANS + k * PER_SCAN)
                sp.dma_start(x_tok[:, :, :].bitcast(I32), of_batch(scan_v[k], b)).then_inc(scan_loaded, 16)

            def batch(b, first, ahead):
                jobs = jobs_of(b, first, ahead)
                if not first:
                    wait_alone(sp, scanned, b * SCANS)
                if ahead:
                    sp.dma_start(x_tok[:, :, :], of_batch(x_v, b + 1)).then_inc(x_loaded, 16)
                else:
                    sp.wait_ge(y1_stored, 16 * NT)
                    sp.dma_start(x_tok[:, :, :], y1_v[0]).then_inc(x_loaded, 16)
                for g in range(NG):
                    if ("k", g + 2) in jobs.place:
                        stack(jobs, b, g + 2)
                    if g == 1:
                        for c in range(ND - 2, ND):
                            wait_alone(sp, pj_full[jobs.bank("x", c)], jobs.done("x", c))
                        load_scan(b, 0)
                        if not first:
                            store_y1(b - 1)
                    if g == 2:
                        load_scan(b, 1)
                        if not first:
                            wait_alone(sp, y1_stored, b * (16 * NT))
                            sp.dma_start(z_tok[:, :, :], of_batch(x_v, b)).then_inc(z_loaded, 16)
                        load_scan(b, 2)

            batch(0, True, True)
            with sp.Fori(1, B - 1) as b:
                batch(b, False, True)
            batch(B - 1, False, False)

            def load_piece(m):
                kind, n = WEIGHTS[m][:2]
                if m >= INTS:
                    sp.wait_ge(fw_shifted, m - INTS + 1)
                src = gate_v[n] if kind == "g" else up_v[n] if kind == "u" else down_v[n, WEIGHTS[m][2]]
                sp.dma_start(w_int[:, m % INTS, :], src).then_inc(fw_loaded[m % INTS], 16)

            sp.wait_ge(score_full, B * UNITS * HG)
            for m in range(INTS):
                load_piece(m)
            with nc.allow_non_contiguous_dma(reason="a scale per partition"):
                sp.dma_start(g_scale[:, :], gate_scale.rearrange("(c p) -> p c", p=P)).then_inc(scales_loaded, 16)
                sp.dma_start(u_scale[:, :], up_scale.rearrange("(c p) -> p c", p=P)).then_inc(scales_loaded, 16)
            sp.dma_start(d_scale[:, :], down_scale.partition_broadcast(P)).then_inc(scales_loaded, 16)
            sp.wait_ge(scanned, B * SCANS)
            sp.dma_start(x_tok[:, :, :], y1_v[1]).then_inc(y_loaded, 16)
            for m in range(INTS, len(WEIGHTS)):
                load_piece(m)
            store_y1(B - 1)
            sp.wait_ge(y1_stored, 16 * B * NT)
            sp.dma_start(z_tok[:, :, :], y1_v[0]).then_inc(r_loaded, 16)

            def store_out(b):
                for t in range(NT):
                    wait_alone(sp, out_done, b * NT + t + 1)
                    sp.dma_start(of_batch(out_v, b)[:, t, :], z_tok[:, t, :]).then_inc(out_stored, 16)

            def ffn_batch(b, ahead):
                if ahead:
                    wait_alone(sp, yT_kept, b * ND)
                    sp.dma_start(x_tok[:, :, :], of_batch(y1_v, b + 1)).then_inc(y_loaded, 16)
                store_out(b - 1)
                wait_alone(sp, out_stored, b * (16 * NT))
                sp.dma_start(z_tok[:, :, :], of_batch(y1_v, b)).then_inc(r_loaded, 16)

            with sp.Fori(1, B - 1) as b:
                ffn_batch(b, True)
            ffn_batch(B - 1, False)
            store_out(B - 1)
            sp.wait_ge(out_stored, 16 * B * NT)

        @block.gpsimd
        def _(pool):
            nc.gpsimd.memset(ident[:, :], 0.0)
            nc.gpsimd.memset(causal[:, :], 0.0)
            nc.gpsimd.memset(minus_exact[:, :], 1.0 - EXACT)
            nc.gpsimd.memset(half_power[:, :], -0.5).then_inc(pool_step, 1)
            pool.wait_ge(pool_step, 1)
            nc.gpsimd.affine_select(out=ident[:, :], in_=ident[:, :], compare_op=ALU.not_equal, fill=1.0, base=0,
                                    pattern=[[-1, P]], channel_multiplier=1)
            nc.gpsimd.affine_select(out=causal[:, S - P:S], in_=causal[:, S - P:S], compare_op=ALU.is_ge, fill=FLOOR,
                                    base=0, pattern=[[-1, P]], channel_multiplier=1).then_inc(consts_ready, 1)
            pool.wait_ge(bias_loaded, 16 * (HG + 2))

            def root(b, var, rstd):
                pool.wait_ge(var, b + 1)
                nc.gpsimd.tensor_tensor(ln_rstd[:, :], ln_var[:, :], half_power[:, :], ALU.pow).then_inc(rstd, 1)

            def apply_norm(b, t):
                if t == 0:
                    root(b, var_done, rstd_done)
                    wait_alone(pool, rstd_done, b + 1)
                nc.gpsimd.tensor_scalar(z_tok[:, t, :], z_tok[:, t, :], ln_mv[:, t, 0:1], ln_rstd[:, t:t + 1],
                                        ALU.subtract, ALU.mult).then_inc(y1_done, 1)

            def att_lo(b, g):
                pool.wait_ge(att_hi_done, b * NG + g + 1)
                nc.gpsimd.tensor_tensor(attT_lo[:, g, :], attT[:, :], attT_hi[:, g, :].bitcast(F32),
                                        ALU.subtract).then_inc(att_ready, 1)

            def batch(b, first):
                for u in range(UNITS):
                    g, qb = divmod(u, NT)
                    wait_alone(pool, inv_done, b * UNITS + u + 1)
                    nc.gpsimd.tensor_copy(inv_wide[:, wide_place(g, qb), :, :],
                                          inv_sum[:, g % 2, qb, :].unsqueeze(2).broadcast_to((P, HG, HD))).then_inc(inv_widened, 1)
                    if g > 0 and qb == 0:
                        att_lo(b, g - 1)
                    if NORM_AT <= u < NORM_AT + NT and not first:
                        apply_norm(b - 1, u - NORM_AT)
                    if u == UNITS - 2:
                        pool.wait_ge(z_loaded, b * 16 + 16)
                        for t in range(NT):
                            last = nc.gpsimd.tensor_tensor(z_tok[:, t, :], z_tok[:, t, :], bias_o[:, :], ALU.add)
                        last.then_inc(res_ready, 1)
                att_lo(b, NG - 1)

            batch(0, True)
            with pool.Fori(1, B) as b:
                batch(b, False)
            pool.wait_ge(scan_rows_done, 1)
            nc.gpsimd.tensor_reduce(scan_top[:, :], scan_rows[:, :], mybir.AxisListType.XYZWC, ALU.max).then_inc(scan_top_done, 1)
            pool.wait_ge(scan_top_done, 1)
            nc.gpsimd.tensor_scalar(wide_flag[:, :], scan_top[:, :], 0.0, None, ALU.is_gt).then_inc(scan_done, 1)
            for t in range(NT):
                apply_norm(B - 1, t)
            with pool.Fori(0, B - 1) as b:
                root(b, var2_done, rstd2_done)
            for t in range(NT):
                pool.wait_ge(var2_done, B + t)
                nc.gpsimd.tensor_tensor(ln_rstd[:, t:t + 1], ln_var[:, t:t + 1], half_power[:, t:t + 1],
                                        ALU.pow).then_inc(rstd2_done, 1)

        @block.scalar
        def _(act):
            act.wait_ge(consts_ready, 1)
            nc.scalar.activation(ln_rstd[:, :], half_power[:, :], ACT.Exp).then_inc(pT_evicted[0], 1)
            with act.Fori(0, NROUND // 2) as r:
                for s in range(TPR):
                    act.wait_ge(w_full, r * TPR + s + 1)
                    nc.scalar.activation(by_row(wT_hi, r * (TPR * P) + s * P),
                                         w_bank[s][:, :].rearrange("p (c j d) -> p c j d", c=ND, j=HG),
                                         ACT.Copy).then_inc(w_hi_done, 1)
            act.wait_ge(bias_loaded, 16 * (HG + 2))

            def x_hi(jobs, c):
                act.wait_ge(pj_full[jobs.bank("x", c)], jobs.done("x", c))
                nc.scalar.activation(xT_hi[:, c, :], pj[jobs.bank("x", c)][:, :], ACT.Copy).then_inc(x_hi_done, 1)

            def qk_hi(jobs, b, kind, r):
                n = "qk".index(kind)
                act.wait_ge(pj_full[jobs.bank(kind, r)], jobs.done(kind, r))
                if r >= 1:
                    act.wait_ge(stacked, (b * NG + r) * STACK_DMAS)
                chunk = n * NG + r % NG
                nc.scalar.activation((q_hi, k_hi)[n][:, :], pj[jobs.bank(kind, r)][:, :], ACT.Identity,
                                     bias=bias_qk[:, chunk:chunk + 1]).then_inc(qk_hi_done, 1)

            def exponentials(b, u, j):
                act.wait_ge(neg_done, b * UNITS + u + 1)
                qb = u % NT
                nc.scalar.activation(probs[qb][:, j, :], probs[qb][:, j, :], ACT.Exp, bias=neg_max[:, qb, j:j + 1],
                                     scale=SCALE, accum_out=row_sum[:, qb, j:j + 1]).then_inc(exp_done, 1)

            def place_values(b, first, t):
                if not first:
                    act.wait_ge(pv_full, b * NG)
                jobs = front_jobs if first else jobs_before(b)
                act.wait_ge(pj_drained[jobs.bank("v", t)], jobs.done("v", t))
                nc.scalar.activation(v_tok[:, t, :], v_next[:, t, :], ACT.Copy).then_inc(v_placed, 1)

            def keep_inverse(jobs, b, g):
                act.wait_ge(pj_full[jobs.bank("r", g)], jobs.done("r", g))
                nc.scalar.activation(invT[:, :], pj[jobs.bank("r", g)][:, :], ACT.Copy).then_inc(inv_kept, 1)

            def att_hi(jobs, b, g):
                act.wait_ge(pj_drained[jobs.bank("r", g)], jobs.done("r", g))
                nc.scalar.activation(attT_hi[:, g, :], attT[:, :], ACT.Copy).then_inc(att_hi_done, 1)

            for c in range(ND):
                x_hi(front_jobs, c)
            for r in range(2):
                if r == 1:
                    with act.Fori(NROUND // 2, NROUND) as r2:
                        for s in range(TPR):
                            act.wait_ge(w_full, r2 * TPR + s + 1)
                            nc.scalar.activation(wT_hi[:, :, bass.ds(r2 * (TPR * P) + s * P, P)],
                                                 w_bank[s][:, :].rearrange("p (c e) -> p c e", c=ND),
                                                 ACT.Copy).then_inc(w_hi_done, 1)
                for kind in "qk":
                    qk_hi(front_jobs, 0, kind, r)
                    if r == 1 and kind == "q":
                        for j in range(HG):
                            exponentials(0, 0, j)

            def scan(b, n):
                act.wait_ge(scan_loaded, (b * len(scan_v) + n // PER_SCAN + 1) * 16)
                if n or not (isinstance(b, int) and b == 0):
                    act.wait_ge(scanned, b * SCANS + n)
                w = NT // PER_SCAN
                t = n % PER_SCAN * w
                nc.scalar.activation(scan_excess[:, :], x_tok[:, t:t + w, :].rearrange("p t d -> p (t d)").bitcast(U32),
                                     ACT.Relu, bias=minus_exact[:, 0:1],
                                     accum_out=scan_sums[:, bass.ds(b * SCANS + n, 1)]).then_inc(scanned, 1)

            def batch(b, first, ahead):
                jobs, over = jobs_of(b, first, ahead), filled(first, ahead)
                for u in range(UNITS):
                    g, qb = divmod(u, NT)
                    for j in range(HG):
                        s = qb * HG + j
                        for kind, n in over.get(u * HG + j, []):
                            if kind in "qk":
                                qk_hi(jobs, b, kind, n)
                        if j <= qb and block_of(u, j) % 2 == 0:
                            evict_block(act, 0, b, block_of(u, j),
                                        lambda o, i: nc.scalar.activation(o, i, ACT.Copy))
                        if g > 0 and s == 0:
                            keep_inverse(jobs, b, g - 1)
                        if j < HG // 2 and (ahead or u + 1 < UNITS):
                            exponentials(b, u + 1, 2 * j)
                            exponentials(b, u + 1, 2 * j + 1)
                        if u * HG + j == 1 and not first:
                            att_hi(jobs_before(b), b - 1, NG - 1)
                        if u * HG + j in PLACE_STEPS[0 if first else 1:]:
                            place_values(b, first, PLACE_STEPS.index(u * HG + j))
                        if g > 0 and s == 2:
                            att_hi(jobs, b, g - 1)
                        if g == NG - 3 and s in X_STEPS:
                            x_hi(jobs, X_STEPS.index(s))
                        if u * HG + j in LATE_SCAN_STEPS and not first:
                            scan(b - 1, len(SCAN_STEPS) + LATE_SCAN_STEPS.index(u * HG + j))
                        if u * HG + j in SCAN_STEPS:
                            scan(b, SCAN_STEPS.index(u * HG + j))
                keep_inverse(jobs, b, NG - 1)
                if ahead:
                    place_values(b + 1, False, 0)
                else:
                    att_hi(jobs, b, NG - 1)
                for n in range(len(SCAN_STEPS), 0 if ahead else SCANS):
                    scan(b, n)

            batch(0, True, True)
            with act.Fori(1, B - 1) as b:
                batch(b, False, True)
            batch(B - 1, False, False)

            def evict_piece(n, weights):
                act.wait_ge(piece_full, n + 1)
                nc.scalar.activation(piece_place(PIECES[n], weights),
                                     piece_bank[n % 2][:, :].rearrange("p (c e) -> p c e", c=TPR),
                                     ACT.Copy).then_inc(piece_evicted(PIECES[n])[0], 1)

            def gate_out(b, i, bank):
                act.wait_ge(gate_full, b * NI + i + 1)
                nc.scalar.activation(silu[:, i % 2, :], bank[:, :], ACT.Silu,
                                     scale=g_scale[:, i:i + 1]).then_inc(silu_done, 1)

            def hidden_hi(b, i):
                act.wait_ge(hid_done, b * NI + i + 1)
                nc.scalar.activation(hid_hi[:, i % HIDS, :], hid[:, i % 2, :], ACT.Copy).then_inc(hid_hi_done, 1)

            def y_hi(b):
                act.wait_ge(up_full, (b + 1) * NI)
                for c in range(ND):
                    act.wait_ge(yT_kept, b * ND + c + 1)
                    nc.scalar.activation(xT_hi[:, c, :], yT_next[:, c, :], ACT.Copy).then_inc(yT_hi_done, 1)

            def first_batch(weights):
                for n in range(len(FIRST_PIECES)):
                    evict_piece(n, weights)
                act.wait_ge(scales_loaded, 48)
                n = len(FIRST_PIECES)
                for i in range(NI):
                    gate_out(0, i, gate_acc[0])
                    evict_piece(n, weights)
                    hidden_hi(0, i)
                    for m in range(1, len(pieces_at(i))):
                        evict_piece(n + m, weights)
                    n += len(pieces_at(i))

            act.wait_ge(scan_done, 1)
            wide = act.value_load(wide_flag[0:1, 0:1], min_val=0, max_val=1)
            with act.If(wide < 1):
                first_batch(exact_weights)
            with act.If(wide > 0):
                first_batch(wide_weights)
            y_hi(0)

            def ffn_batch(b, ahead):
                turns = turns_of(ahead)
                for n, i in enumerate(turns):
                    if isinstance(i, tuple):
                        for c in (i[1], i[1] + 1):
                            act.wait_ge(yT_full, (b - 1) * ND + c + 1)
                            nc.scalar.activation(yT_next[:, c, :], (gate_acc, up_acc)[c % 2][n % 2][:, :],
                                                 ACT.Copy).then_inc(yT_kept, 1)
                    else:
                        gate_out(b, i, gate_acc[n % 2])
                        hidden_hi(b, i)
                if ahead:
                    y_hi(b)

            with act.Fori(1, B - 1) as b:
                ffn_batch(b, True)
            ffn_batch(B - 1, False)

        @block.vector
        def _(dve):
            nc.vector.memset(ln_stat[:, :, :], 0.0).then_inc(pT_evicted[1], 1)
            nc.vector.memset(ln_mv[:, :, :], 0.0).then_inc(d_done, 1)
            with dve.Fori(0, NROUND // 2) as r:
                for s in range(TPR):
                    first = r * (TPR * P) + s * P
                    dve.wait_ge(w_hi_done, r * TPR + s + 1)
                    nc.vector.tensor_tensor(by_row(wT_lo, first),
                                            w_bank[s][:, :].rearrange("p (c j d) -> p c j d", c=ND, j=HG),
                                            by_row(wT_hi, first).bitcast(F32), ALU.subtract).then_inc(w_free, 1)
            dve.wait_ge(bias_loaded, 16 * (HG + 2))
            dve.wait_ge(consts_ready, 1)

            def x_lo(jobs, count, c):
                dve.wait_ge(x_hi_done, count + c + 1)
                nc.vector.tensor_tensor(xT_lo[:, c, :], pj[jobs.bank("x", c)][:, :], xT_hi[:, c, :].bitcast(F32),
                                        ALU.subtract).then_inc(pj_drained[jobs.bank("x", c)], 1)

            def qk_lo(jobs, b, kind, r):
                n = "qk".index(kind)
                chunk = n * NG + r % NG
                dve.wait_ge(qk_hi_done, (b * NG + r) * 2 + n + 1)
                nc.vector.scalar_tensor_tensor(
                    out=(q_lo, k_lo)[n][:, :], in0=pj[jobs.bank(kind, r)][:, :], scalar=bias_qk[:, chunk:chunk + 1],
                    in1=(q_hi, k_hi)[n][:, :].bitcast(F32), op0=ALU.add,
                    op1=ALU.subtract).then_inc(pj_drained[jobs.bank(kind, r)], 1)

            def values(jobs, t):
                dve.wait_ge(pj_full[jobs.bank("v", t)], jobs.done("v", t))
                nc.vector.tensor_tensor(v_next[:, t, :], pj[jobs.bank("v", t)][:, :], bias_v[:, :],
                                        ALU.add).then_inc(pj_drained[jobs.bank("v", t)], 1)

            def tile_max(b, u, j):
                qb = u % NT
                w = P_WIDTH[qb]
                wait_alone(dve, score_full, (b * UNITS + u) * HG + j + 1)
                nc.vector.tensor_tensor_reduce(
                    out=probs[qb][:, j, :], in0=score[j % 2][:, 0:w], in1=causal[:, S - w:S], scale=1.0, scalar=FLOOR,
                    op0=ALU.add, op1=ALU.max, accum_out=row_max[:, qb, j:j + 1]).then_inc(max_done, 1)

            def negate_max(b, u):
                qb = u % NT
                dve.wait_ge(max_done, (b * UNITS + u + 1) * HG)
                nc.vector.tensor_scalar(neg_max[:, qb, :], row_max[:, qb, :], -SCALE, None, ALU.mult).then_inc(neg_done, 1)

            def inverse_sum(b, u):
                qb = u % NT
                dve.wait_ge(exp_done, (b * UNITS + u + 1) * HG)
                nc.vector.reciprocal(inv_sum[:, u // NT % 2, qb, :], row_sum[:, qb, :]).then_inc(inv_done, 1)

            def normalise(jobs, b, g):
                dve.wait_ge(inv_kept, b * NG + g + 1)
                dve.wait_ge(pv_full, b * NG + g + 1)
                nc.vector.tensor_tensor(attT[:, :], pv_acc[g % 2][:, :], invT[:, :], ALU.mult).then_inc(pj_drained[jobs.bank("r", g)], 1)

            def statistics(b, t, stat, mv):
                nc.vector.bn_stats(ln_stat[:, t, :], z_tok[:, t, :]).then_inc(stat, 1)
                wait_alone(dve, stat, b * NT + t + 1)
                nc.vector.bn_aggr(ln_mv[:, t, :], ln_stat[:, t, :]).then_inc(mv, 1)

            def variance(b, mv, var):
                dve.wait_ge(mv, (b + 1) * NT)
                nc.vector.tensor_scalar(ln_var[:, :], ln_mv[:, :, 1], EPS, None, ALU.add).then_inc(var, 1)

            def apply_norm(b, t, rstd, done):
                dve.wait_ge(rstd, b + 1)
                nc.vector.tensor_scalar(z_tok[:, t, :], z_tok[:, t, :], ln_mv[:, t, 0:1], ln_rstd[:, t:t + 1],
                                        ALU.subtract, ALU.mult).then_inc(done, 1)

            for c in range(ND):
                x_lo(front_jobs, 0, c)
            for kind in "qk":
                qk_lo(front_jobs, 0, kind, 0)
            with dve.Fori(NROUND // 2, NROUND) as r:
                for s in range(TPR):
                    col = bass.ds(r * (TPR * P) + s * P, P)
                    dve.wait_ge(w_hi_done, r * TPR + s + 1)
                    nc.vector.tensor_tensor(wT_lo[:, :, col], w_bank[s][:, :].rearrange("p (c e) -> p c e", c=ND),
                                            wT_hi[:, :, col].bitcast(F32), ALU.subtract).then_inc(w_free, 1)
            for t in range(NT):
                values(front_jobs, t)
            for u in range(AHEAD):
                for j in range(HG):
                    tile_max(0, u, j)
                negate_max(0, u)
                qk_lo(front_jobs, 0, "qk"[u], 1)
            inverse_sum(0, 0)

            def outputs(jobs, kind, b, t):
                dve.wait_ge(pj_full[jobs.bank(kind, t)], jobs.done(kind, t))
                if t == 0:
                    dve.wait_ge(res_ready, b + 1)
                nc.vector.tensor_tensor(z_tok[:, t, :], pj[jobs.bank(kind, t)][:, :], z_tok[:, t, :],
                                        ALU.add).then_inc(pj_drained[jobs.bank(kind, t)], 1)

            def output_statistics(jobs, kind, b, t):
                dve.wait_ge(pj_drained[jobs.bank(kind, t)], jobs.done(kind, t))
                statistics(b, t, stat_done, mv_done)

            def shift_piece(m):
                dve.wait_ge(fw_loaded[m % INTS], 16 * (m // INTS + 1))
                if m >= SHIFTS:
                    dve.wait_ge(piece_full, PIECES.index(WEIGHTS[m - SHIFTS]) + 1)
                nc.vector.tensor_scalar(w_shift[:, m % SHIFTS, :], w_int[:, m % INTS, :], -ZERO_POINT, None,
                                        ALU.add).then_inc(fw_shifted, 1)

            def take(jobs, b, over):
                for kind, n in over:
                    if kind == "v":
                        values(jobs, n)
                    if kind == "o":
                        outputs(jobs, kind, b - 1, n)

            def batch(b, first, ahead):
                jobs, over = jobs_of(b, first, ahead), filled(first, ahead)
                for u in range(UNITS):
                    g, qb = divmod(u, NT)
                    for j in range(HG):
                        s = qb * HG + j
                        take(jobs, b, over.get(u * HG + j, []))
                        if ahead or u + AHEAD < UNITS:
                            tile_max(b, u + AHEAD, j)
                        if j <= qb and block_of(u, j) % 2 == 1:
                            evict_block(dve, 1, b, block_of(u, j), nc.vector.tensor_copy)
                        if j == 2 and (ahead or u + 1 < UNITS):
                            inverse_sum(b, u + 1)
                        if g > 0 and s == 1:
                            normalise(jobs, b, g - 1)
                        for kind, n in over.get(u * HG + j, []):
                            if kind in "qk":
                                qk_lo(jobs, b, kind, n)
                            if kind == "o":
                                output_statistics(jobs, kind, b - 1, n)
                        if g == NG - 3 and s - 1 in X_STEPS:
                            x_lo(jobs, (b + 1) * ND, X_STEPS.index(s - 1))
                    if ahead or u + AHEAD < UNITS:
                        negate_max(b, u + AHEAD)
                    if u == NORM_AT - 1 and not first:
                        variance(b - 1, mv_done, var_done)
                take(jobs, b, over.get(UNITS * HG, []))
                normalise(jobs, b, NG - 1)
                if not ahead:
                    for m in range(SHIFTS):
                        shift_piece(m)
                    dve.wait_ge(scanned, B * SCANS)
                    nc.vector.tensor_reduce(scan_rows[:, :], scan_sums[:, :], mybir.AxisListType.X, ALU.max).then_inc(scan_rows_done, 1)
                    for t in range(NT):
                        outputs(jobs, "f", b, t)
                        output_statistics(jobs, "f", b, t)

            batch(0, True, True)
            with dve.Fori(1, B - 1) as b:
                batch(b, False, True)
            batch(B - 1, False, False)

            def hidden(b, i, bank):
                dve.wait_ge(up_full, b * NI + i + 1)
                dve.wait_ge(silu_done, b * NI + i + 1)
                nc.vector.scalar_tensor_tensor(out=hid[:, i % 2, :], in0=bank[:, :], scalar=u_scale[:, i:i + 1],
                                               in1=silu[:, i % 2, :], op0=ALU.mult, op1=ALU.mult).then_inc(hid_done, 1)
                dve.wait_ge(hid_hi_done, b * NI + i + 1)
                nc.vector.tensor_tensor(hid_lo[:, i % HIDS, :], hid[:, i % 2, :], hid_hi[:, i % HIDS, :].bitcast(F32),
                                        ALU.subtract).then_inc(hid_ready, 1)

            def y_lo(b):
                for c in range(ND):
                    dve.wait_ge(yT_hi_done, b * ND + c + 1)
                    nc.vector.tensor_tensor(xT_lo[:, c, :], yT_next[:, c, :], xT_hi[:, c, :].bitcast(F32),
                                            ALU.subtract).then_inc(yT_done, 1)

            def drain_down(b, t):
                dve.wait_ge(down_full, (b + 1) * NI - (NT - 1 - t if isinstance(b, int) and b == LAST else 0))
                nc.vector.tensor_tensor(d_scaled[:, t, :], down_acc[t][:, :], d_scale[:, :], ALU.mult).then_inc(d_done, 1)

            def add_residual(b, t):
                dve.wait_ge(d_done, b * NT + t + 2)
                nc.vector.tensor_tensor(z_tok[:, t, :], d_scaled[:, t, :], z_tok[:, t, :], ALU.add).then_inc(z2_done, 1)
                dve.wait_ge(z2_done, b * NT + t + 1)
                statistics(b, t, stat2_done, mv2_done)

            def finish(b):
                dve.wait_ge(r_loaded, b * 16 + 16)
                for t in range(NT):
                    add_residual(b, t)
                    yield
                variance(b, mv2_done, var2_done)
                yield
                for t in range(NT):
                    apply_norm(b, t, rstd2_done, out_done)
                    yield

            for m in range(SHIFTS, len(FIRST_PIECES)):
                shift_piece(m)
            m = len(FIRST_PIECES)
            variance(B - 1, mv_done, var_done)
            dve.wait_ge(scales_loaded, 48)
            for i in range(NI):
                for piece in pieces_at(i):
                    if piece in WEIGHTS:
                        shift_piece(m)
                        m += 1
                hidden(0, i, up_acc[0])
            y_lo(0)
            for t in range(NT):
                drain_down(0, t)

            def ffn_batch(b, ahead):
                steps = finish(b - 1)
                for n, i in enumerate(turns_of(ahead)):
                    if not isinstance(i, tuple):
                        hidden(b, i, up_acc[n % 2])
                        next(steps, None)
                if ahead:
                    y_lo(b)
                    for t in range(NT):
                        drain_down(b, t)

            with dve.Fori(1, B - 1) as b:
                ffn_batch(b, True)
            ffn_batch(B - 1, False)
            dve.wait_ge(r_loaded, LAST * 16 + 16)
            for t in range(NT):
                drain_down(LAST, t)
                add_residual(LAST, t)
                dve.wait_ge(mv2_done, LAST * NT + t + 1)
                nc.vector.tensor_scalar(ln_var[:, t:t + 1], ln_mv[:, t, 1:2], EPS, None, ALU.add).then_inc(var2_done, 1)
                if t > 0:
                    apply_norm(LAST + t - 1, t - 1, rstd2_done, out_done)
            apply_norm(LAST + NT - 1, NT - 1, rstd2_done, out_done)

        @block.tensor
        def _(pe):
            pe.wait_ge(consts_ready, 1)

            def transpose_weights(r):
                for s in range(TPR):
                    pe.wait_ge(w_loaded[r] if r else w_first[s], 16)
                    if r >= 1:
                        pe.wait_ge(w_free, (r - 1) * TPR + s + 1)
                    for c in range(ND):
                        last = nc.tensor.transpose(w_bank[s][:, c * P:(c + 1) * P], w_stage[r][:, s, c * P:(c + 1) * P],
                                                   ident[:, :])
                    last.then_inc(w_full, 1)

            def bank_for(jobs, *job):
                if jobs.before_it(*job) is not None:
                    pe.wait_ge(pj_drained[jobs.bank(*job)], jobs.before_it(*job))
                return pj[jobs.bank(*job)]

            def transpose_x(jobs, b, c):
                if c == 0:
                    pe.wait_ge(x_loaded, b * 16 + 16)
                acc = bank_for(jobs, "x", c)
                for t in range(NT):
                    last = nc.tensor.transpose(acc[:, t * P:(t + 1) * P], x_tok[:, t, c * P:(c + 1) * P], ident[:, :])
                last.then_inc(pj_full[jobs.bank("x", c)], 1)

            def project(jobs, x_jobs, r):
                for n, kind in enumerate("qk"):
                    acc = bank_for(jobs, kind, r)
                    e = slice(n * D + r % NG * P, n * D + (r % NG + 1) * P)
                    for c in range(ND):
                        if x_jobs is not None and n == 0:
                            pe.wait_ge(pj_drained[x_jobs.bank("x", c)], x_jobs.done("x", c))
                        first, final = c == 0, c == ND - 1
                        nc.tensor.matmul(acc[:, :], wT_hi[:, c, e], xT_hi[:, c, :], start=first, stop=False)
                        yield
                        nc.tensor.matmul(acc[:, :], wT_hi[:, c, e], xT_lo[:, c, :], start=False, stop=False)
                        yield
                        last = nc.tensor.matmul(acc[:, :], wT_lo[:, c, e], xT_hi[:, c, :], start=False, stop=final)
                        if final:
                            last.then_inc(pj_full[jobs.bank(kind, r)], 1)
                        yield

            def project_values(jobs, t):
                acc = bank_for(jobs, "v", t)
                tok = slice(t * P, (t + 1) * P)
                for c in range(ND):
                    for n, (a, w) in enumerate(((xT_hi, wT_hi), (xT_hi, wT_lo), (xT_lo, wT_hi))):
                        last = nc.tensor.matmul(acc[:, :], a[:, c, tok], w[:, c, 2 * D:3 * D], start=c == 0 and n == 0,
                                                stop=c == ND - 1 and n == 2)
                        if c == ND - 1 and n == 2:
                            last.then_inc(pj_full[jobs.bank("v", t)], 1)
                        yield

            def scores(b, u, j):
                r, qb = divmod(u, NT)
                n = (b * UNITS + u) * HG + j
                w = P_WIDTH[qb]
                if qb == 0 and j == 0:
                    pe.wait_ge(stacked, (b * NG + r + 1) * STACK_DMAS)
                if u > 0 or j >= 2:
                    pe.wait_ge(max_done, n - 1)
                nc.tensor.matmul(score[j % 2][:, 0:w], q_stack[r % 2][:, j, qb * P:(qb + 1) * P],
                                 k_stack[r % 2][:, j, 0:w], start=True, stop=True).then_inc(score_full, 1)

            def transpose_block(b, u, kb):
                n = block_of(u, kb)
                qb = u % NT
                pe.wait_ge(pT_evicted[n % 2], b * (NG * BLOCKS // 2) + n // 2 + 1)
                for j in range(HG):
                    if kb == 0:
                        pe.wait_ge(exp_done, (b * UNITS + u) * HG + j + 1)
                    last = nc.tensor.transpose(pT[n % 2][:, j * P:(j + 1) * P], probs[qb][:, j, kb * P:(kb + 1) * P],
                                               ident[:, :])
                last.then_inc(pT_full, 1)

            def weighted_values(jobs, first, b, u, kb):
                n = block_of(u, kb)
                g, qb = divmod(u, NT)
                if qb == 0 and not (first and g < 2):
                    old, r = (jobs, g - 2) if g >= 2 else (jobs_before(b), g - 2 + NG)
                    pe.wait_ge(pj_drained[old.bank("r", r)], old.done("r", r))
                if g == 0 and kb == qb:
                    pe.wait_ge(v_placed, b * NT + kb + 1)
                pe.wait_ge(pT_evicted[n % 2], b * (NG * BLOCKS // 2) + n // 2 + 2)
                for j in range(HG):
                    h = g * HG + j
                    last = nc.tensor.matmul(pv_acc[g % 2][j * HD:(j + 1) * HD, qb * P:(qb + 1) * P],
                                            v_tok[:, kb, h * HD:(h + 1) * HD], probsT[:, n % 2, j, :],
                                            start=kb == 0, stop=kb == qb)
                if qb == NT - 1 and kb == qb:
                    last.then_inc(pv_full, 1)

            def transpose_inverse(jobs, b, g):
                acc = bank_for(jobs, "r", g)
                pe.wait_ge(inv_widened, b * UNITS + (g + 1) * NT)
                for qb in range(NT):
                    last = nc.tensor.transpose(acc[:, qb * P:(qb + 1) * P],
                                               inv_wide[:, wide_place(g, qb), :, :].rearrange("p j d -> p (j d)"), ident[:, :])
                last.then_inc(pj_full[jobs.bank("r", g)], 1)

            for r in range(NROUND // 2):
                transpose_weights(r)
            for c in range(ND):
                transpose_x(front_jobs, 0, c)
            pe.wait_ge(w_free, NROUND // 2 * TPR)
            for _ in project(front_jobs, front_jobs, 0):
                pass
            for r in range(NROUND // 2, NROUND):
                transpose_weights(r)
            pe.wait_ge(w_free, NROUND * TPR)
            for t in range(NT):
                for _ in project_values(front_jobs, t):
                    pass
            work = project(front_jobs, None, 1)
            for u in range(AHEAD):
                for j in range(HG):
                    scores(0, u, j)
                    for _ in range(3):
                        next(work)
            next(work, None)

            def project_out(jobs, kind, b, t):
                acc = bank_for(jobs, kind, t)
                tok = slice(t * P, (t + 1) * P)
                for c in range(NG):
                    if t == 0:
                        pe.wait_ge(att_ready, b * NG + c + 1)
                    for n, (a, w) in enumerate(((attT_hi, wT_hi), (attT_hi, wT_lo), (attT_lo, wT_hi))):
                        last = nc.tensor.matmul(acc[:, :], a[:, c, tok], w[:, c, NE:NE + D], start=c == 0 and n == 0,
                                                stop=c == NG - 1 and n == 2)
                        if c == NG - 1 and n == 2:
                            last.then_inc(pj_full[jobs.bank(kind, t)], 1)
                        yield

            def batch(b, first, ahead):
                jobs = jobs_of(b, first, ahead)
                waiting = None
                for u in range(UNITS):
                    g, qb = divmod(u, NT)
                    if qb == 0:
                        spread, counts = filling(first, ahead, g)
                        work = chain(project(jobs, jobs if g + 2 == NG else None, g + 2) if spread else [],
                                     *(project_out(jobs, "o", b - 1, t) for kind, t in spread if kind == "o"),
                                     *(project_values(jobs, t) for kind, t in spread if kind == "v"))
                    for j in range(HG):
                        s = qb * HG + j
                        if ahead or u + AHEAD < UNITS:
                            scores(b, u + AHEAD, j)
                        if j <= qb:
                            transpose_block(b, u, j)
                        for _ in range(counts[s]):
                            next(work)
                        if waiting:
                            weighted_values(jobs, first, b, *waiting)
                        waiting = (u, j) if j <= qb else None
                        if g == NG - 3 and s in X_STEPS:
                            transpose_x(jobs, b + 1, X_STEPS.index(s))
                    if qb == NT - 1:
                        transpose_inverse(jobs, b, g)
                weighted_values(jobs, first, b, *waiting)
                if not ahead:
                    for t in range(NT):
                        for _ in project_out(jobs, "f", b, t):
                            pass

            batch(0, True, True)
            with pe.Fori(1, B - 1) as b:
                batch(b, False, True)
            batch(B - 1, False, False)

            def ffn(w_gate, w_up, w_down, form):
                last_jobs = jobs_of(B - 1, False, False)

                def transpose_y(b, c, acc):
                    if c == 0:
                        pe.wait_ge(y_loaded, b * 16)
                    for t in range(NT):
                        last = nc.tensor.transpose(acc[:, t * P:(t + 1) * P], x_tok[:, t, c * P:(c + 1) * P], ident[:, :])
                    return last

                def transpose_piece(n):
                    piece = PIECES[n]
                    if n >= 2:
                        pe.wait_ge(*piece_evicted(PIECES[n - 2]))
                    acc = piece_bank[n % 2]
                    if piece[0] == "y":
                        transpose_y(1, piece[1], acc).then_inc(piece_full, 1)
                        return
                    m = WEIGHTS.index(piece)
                    pe.wait_ge(fw_shifted, m + 1)
                    for c in range(TPR):
                        last = nc.tensor.transpose(acc[:, c * P:(c + 1) * P], w_shift[:, m % SHIFTS, c * P:(c + 1) * P],
                                                   ident[:, :])
                    last.then_inc(piece_full, 1)

                def gate_up(b, i, n, arrived):
                    cols = slice(i * P, (i + 1) * P)
                    for kind, w, acc, full in (("g", w_gate, gate_acc, gate_full), ("u", w_up, up_acc, up_full)):
                        if isinstance(b, int) and b == 0:
                            pe.wait_ge(*piece_evicted((kind, i)))
                        for c in range(ND):
                            if i == 0 and kind == "g":
                                arrived(c)
                            nc.tensor.matmul(acc[n][:, :], w[:, c, cols], form(xT_hi[:, c, :]), start=c == 0, stop=False)
                            last = nc.tensor.matmul(acc[n][:, :], w[:, c, cols], form(xT_lo[:, c, :]), start=False, stop=c == ND - 1)
                        last.then_inc(full, 1)

                def down_block(b, i, t):
                    tok = slice(t * P, (t + 1) * P)
                    nc.tensor.matmul(down_acc[t][:, :], form(hid_hi[:, i % HIDS, tok]), w_down[:, i, :], start=i == 0, stop=False)
                    return nc.tensor.matmul(down_acc[t][:, :], form(hid_lo[:, i % HIDS, tok]), w_down[:, i, :], start=False,
                                            stop=i == NI - 1)

                def down(b, i):
                    pe.wait_ge(hid_ready, b * NI + i + 1)
                    if i == 0:
                        pe.wait_ge(d_done, b * NT + 1)
                    for t in range(NT):
                        last = down_block(b, i, t)
                    last.then_inc(down_full, 1)

                for t in range(NT - 2, NT):
                    pe.wait_ge(pj_drained[last_jobs.bank("f", t)], last_jobs.done("f", t))
                n = 0
                for piece in FIRST_PIECES:
                    transpose_piece(n)
                    n += 1
                for i in range(NI):
                    if i >= 1:
                        pe.wait_ge(hid_done, i)
                    gate_up(0, i, 0, lambda c: pe.wait_ge(pj_drained[last_jobs.bank("x", c)], last_jobs.done("x", c)))
                    for piece in pieces_at(i)[:-1]:
                        transpose_piece(n)
                        n += 1
                    if i >= 1:
                        if (i - 1) % TPR == 0:
                            pe.wait_ge(*piece_evicted(("d", (i - 1) // TPR, ND - 1)))
                        down(0, i - 1)
                    transpose_piece(n)
                    n += 1
                down(0, NI - 1)
                pe.wait_ge(yT_kept, ND)

                def ffn_batch(b, ahead):
                    turns = turns_of(ahead)
                    for n, i in enumerate(turns):
                        if n >= 2:
                            before = turns[n - 2]
                            if isinstance(before, tuple):
                                pe.wait_ge(yT_kept, b * ND + before[1] + 2)
                            else:
                                pe.wait_ge(hid_done, b * NI + before + 1)
                        if isinstance(i, tuple):
                            for c in (i[1], i[1] + 1):
                                transpose_y(b + 1, c, (gate_acc, up_acc)[c % 2][n % 2]).then_inc(yT_full, 1)
                            continue
                        gate_up(b, i, n % 2, lambda c: pe.wait_ge(yT_done, (b - 1) * ND + c + 1))
                        if i >= 1 and (ahead or i - 1 < NI - NT):
                            down(b, i - 1)
                    if ahead:
                        down(b, NI - 1)

                with pe.Fori(1, B - 1) as b:
                    ffn_batch(b, True)
                ffn_batch(B - 1, False)
                for t in range(2):
                    for i in range(NI - NT, NI - 1):
                        pe.wait_ge(hid_ready, LAST * NI + i + 1)
                        down_block(LAST, i, t)
                pe.wait_ge(hid_ready, LAST * NI + NI)
                for t in range(NT):
                    for i in range(NI - 1 if t < 2 else NI - NT, NI):
                        last = down_block(LAST, i, t)
                    last.then_inc(down_full, 1)

            pe.wait_ge(scan_done, 1)
            wide = pe.value_load(wide_flag[0:1, 0:1], min_val=0, max_val=1)
            with pe.If(wide < 1):
                ffn(*exact_weights, lambda operand: operand)
            with pe.If(wide > 0):
                ffn(*wide_weights, lambda operand: operand.bitcast(F32))


_INS = ['L0_attn_x', 'L0_attn_w_qkv', 'L0_attn_b_qkv', 'L0_attn_w_out', 'L0_attn_b_out', 'L0_ffn_gate_w',
        'L0_ffn_gate_scale', 'L0_ffn_up_w', 'L0_ffn_up_scale', 'L0_ffn_down_w', 'L0_ffn_down_scale']


def kernel(**inputs):
    import numpy as _np
    import concourse.bacc as _bacc
    from concourse import mybir as _mybir
    from concourse.bass_utils import run_bass_kernel_spmd as _run

    nc = _bacc.Bacc("TRN2", target_bir_lowering=False, num_devices=1)
    arrays, args = {}, []
    for name in _INS:
        a = _np.ascontiguousarray(inputs[name])
        arrays[f"in_{name}_dram"] = a
        args.append(nc.dram_tensor(f"in_{name}_dram", a.shape, _mybir.dt.from_np(a.dtype), kind="ExternalInput").ap())
    shape = inputs['L0_attn_x'].shape
    args.append(nc.dram_tensor("out_0_dram", shape, _mybir.dt.float32, kind="ExternalOutput").ap())
    postln_block_kernel(nc, *args)
    r = _run(nc, [arrays], core_ids=[0])
    return r.results[0]["out_0_dram"]
```
